# Optimizing a Trainium2 kernel written in Bass

```python
import numpy as np
import jax
import jax.numpy as jnp

def _softmax(x, axis=-1):
    return jax.nn.softmax(x, axis=axis)

def _gelu(x):
    return jax.nn.gelu(x, approximate=True)

def _silu(x):
    return jax.nn.silu(x)

def _sigmoid(x):
    return jax.nn.sigmoid(x)

def _layernorm(x, axis=-1, eps=1e-05):
    m = jnp.mean(x, axis=axis, keepdims=True)
    v = jnp.var(x, axis=axis, keepdims=True)
    return (x - m) / jnp.sqrt(v + eps)

def _scatter_add(tgt, idx, src, axis=0):
    return tgt.at[idx].add(src)

def _segment_sum(src, seg, n):
    return jax.ops.segment_sum(src, seg, n)
kernel_name = 'mk_adaln_d1_jaxref_r8_82b8c5'

def setup_inputs(seed: int=0):
    np.random.seed(seed)
    _w = jnp.asarray

    def _L0_attn_setup():
        import jax, jax.numpy as jnp
        import numpy as np
        NUM_HEADS = 16
        HEAD_DIM = 64
        NEG_INF = -1000000000.0

        def rotary_embedding(x, seq_len, head_dim):
            positions = jnp.arange(seq_len)
            dim_pairs = jnp.arange(0, head_dim, 2)
            freqs = 1.0 / 10000.0 ** (dim_pairs / head_dim)
            angles = positions[:, None] * freqs[None, :]
            cos = jnp.cos(angles)[:, None, :]
            sin = jnp.sin(angles)[:, None, :]
            x1 = x[..., ::2]
            x2 = x[..., 1::2]
            out1 = x1 * cos - x2 * sin
            out2 = x1 * sin + x2 * cos
            return jnp.stack([out1, out2], axis=-1).reshape(x.shape)
        key = jax.random.key(seed)
        k1, k2, k3 = jax.random.split(key, 3)
        batch, seq_len, embed_dim = (2, 256, 128)
        x = jax.random.normal(k1, (batch, seq_len, embed_dim), dtype=jnp.float32)
        W_qkv = jax.random.normal(k2, (embed_dim, 3 * NUM_HEADS * HEAD_DIM), dtype=jnp.float32) * 0.02
        W_out = jax.random.normal(k3, (NUM_HEADS * HEAD_DIM, embed_dim), dtype=jnp.float32) * 0.02
        return {'x': x, 'W_qkv': W_qkv, 'W_out': W_out}
    _L0_attn_in = _L0_attn_setup()

    def _L0_ffn_setup():
        import jax, jax.numpy as jnp
        import numpy as np
        B, S, H, E, K, I = (4, 256, 128, 8, 2, 512)
        GATE_EPS = 1e-06
        LN_EPS = 1e-05
        key = jax.random.key(seed)
        k0, k1, k2, k3 = jax.random.split(key, 4)
        x = jax.random.normal(k0, (B, S, H), jnp.float32)
        gate_w = jax.random.normal(k1, (E, H), jnp.float32) * np.float32(np.sqrt(2.0 / (H + E)))
        expert_bias = jnp.zeros((E,), jnp.float32)
        w_up = jax.random.normal(k2, (E, I, H), jnp.float32) * np.float32(np.sqrt(2.0 / (H + I)))
        w_down = jax.random.normal(k3, (E, H, I), jnp.float32) * np.float32(np.sqrt(2.0 / (H + I)))
        return {'x': x, 'gate_w': gate_w, 'expert_bias': expert_bias, 'w_up': w_up, 'w_down': w_down}
    _L0_ffn_in = _L0_ffn_setup()
    _L0_c = _w((lambda *s: np.random.randn(*s).astype(np.float32) * 0.05)(8, 128))
    _L0_wmod = _w((lambda *s: np.random.randn(*s).astype(np.float32) * 0.05)(128, 6 * 128) * 128 ** (-0.5))
    _d = {'L0_attn_x': _L0_attn_in['x'], 'L0_attn_W_qkv': _L0_attn_in['W_qkv'], 'L0_attn_W_out': _L0_attn_in['W_out'], 'L0_ffn_gate_w': _L0_ffn_in['gate_w'], 'L0_ffn_expert_bias': _L0_ffn_in['expert_bias'], 'L0_ffn_w_up': _L0_ffn_in['w_up'], 'L0_ffn_w_down': _L0_ffn_in['w_down'], 'L0_c': _L0_c, 'L0_wmod': _L0_wmod}
    _x0 = _d['L0_attn_x']
    _d['L0_attn_x'] = jax.random.normal(jax.random.fold_in(jax.random.key(seed), 1), (8, 512, 128), dtype=_x0.dtype)
    del _x0
    return _d

def reference(L0_attn_x, L0_attn_W_qkv, L0_attn_W_out, L0_ffn_gate_w, L0_ffn_expert_bias, L0_ffn_w_up, L0_ffn_w_down, L0_c, L0_wmod):

    def _L0_attn_ref(x, W_qkv, W_out):
        import jax, jax.numpy as jnp
        import numpy as np
        NUM_HEADS = 16
        HEAD_DIM = 64
        NEG_INF = -1000000000.0

        def rotary_embedding(x, seq_len, head_dim):
            positions = jnp.arange(seq_len)
            dim_pairs = jnp.arange(0, head_dim, 2)
            freqs = 1.0 / 10000.0 ** (dim_pairs / head_dim)
            angles = positions[:, None] * freqs[None, :]
            cos = jnp.cos(angles)[:, None, :]
            sin = jnp.sin(angles)[:, None, :]
            x1 = x[..., ::2]
            x2 = x[..., 1::2]
            out1 = x1 * cos - x2 * sin
            out2 = x1 * sin + x2 * cos
            return jnp.stack([out1, out2], axis=-1).reshape(x.shape)
        batch, seq_len, embed_dim = x.shape
        qkv = jnp.einsum('bse,ef->bsf', x, W_qkv)
        qkv = qkv.reshape(batch, seq_len, 3, NUM_HEADS, HEAD_DIM)
        q, k, v = (qkv[:, :, 0], qkv[:, :, 1], qkv[:, :, 2])
        q = rotary_embedding(q, seq_len, HEAD_DIM)
        k = rotary_embedding(k, seq_len, HEAD_DIM)
        scale = 1.0 / jnp.sqrt(jnp.asarray(HEAD_DIM, dtype=x.dtype))
        scores = jnp.einsum('bqhd,bkhd->bhqk', q, k) * scale
        mask = jnp.tril(jnp.ones((seq_len, seq_len), dtype=bool))[None, None, :, :]
        scores = jnp.where(mask, scores, NEG_INF)
        weights = jax.nn.softmax(scores, axis=-1)
        out = jnp.einsum('bhqk,bkhd->bqhd', weights, v)
        out = out.reshape(batch, seq_len, NUM_HEADS * HEAD_DIM)
        return jnp.einsum('bsf,fe->bse', out, W_out)

    def _L0_ffn_ref(x, gate_w, expert_bias, w_up, w_down):
        import jax, jax.numpy as jnp
        import numpy as np
        B, S, H, E, K, I = (4, 256, 128, 8, 2, 512)
        GATE_EPS = 1e-06
        LN_EPS = 1e-05
        logits = jnp.einsum('bsh,eh->bse', x, gate_w) + expert_bias
        weights = jax.nn.softmax(logits, axis=-1)
        top_w, top_i = jax.lax.top_k(weights, K)
        top_w = top_w / (jnp.sum(top_w, axis=-1, keepdims=True) + GATE_EPS)
        sparse_w = jnp.sum(jax.nn.one_hot(top_i, E, dtype=weights.dtype) * top_w[..., None], axis=-2)
        out = jnp.zeros_like(x)
        for e in range(E):
            h = jax.nn.gelu(jnp.einsum('bsh,ih->bsi', x, w_up[e]), approximate=False)
            y = jnp.einsum('bsi,hi->bsh', h, w_down[e])
            out = out + sparse_w[..., e:e + 1] * y
        mu = jnp.mean(out, axis=-1, keepdims=True)
        var = jnp.mean(jnp.square(out - mu), axis=-1, keepdims=True)
        out = (out - mu) * jax.lax.rsqrt(var + LN_EPS)
        return out + x
    x = L0_attn_x
    mod = (_silu(L0_c) @ L0_wmod).reshape(L0_c.shape[0], 6, 1, -1)
    sa, ca, ga, sb, cb, gb = (mod[:, 0], mod[:, 1], mod[:, 2], mod[:, 3], mod[:, 4], mod[:, 5])
    ga = (2 * (ga >= 0) - 1) * jnp.maximum(jnp.abs(ga), 0.25)
    gb = (2 * (gb >= 0) - 1) * jnp.maximum(jnp.abs(gb), 0.25)
    h = _layernorm(x, axis=-1) * (1 + ca) + sa
    x = x + ga * _L0_attn_ref(h, L0_attn_W_qkv, L0_attn_W_out)
    h = _layernorm(x, axis=-1) * (1 + cb) + sb
    x = x + gb * _L0_ffn_ref(h, L0_ffn_gate_w, L0_ffn_expert_bias, L0_ffn_w_up, L0_ffn_w_down)
    return x

_drawn_inputs = setup_inputs


def setup_inputs(seed=0):
    import zlib

    import numpy as np

    out = dict(_drawn_inputs(seed))
    spreads = {'L0_ffn_expert_bias': (0.0, 0.1)}
    factors = {'L0_attn_W_qkv': 5.764, 'L0_attn_W_out': 6.161}
    for name, (base, spread) in spreads.items():
        noise = np.random.default_rng([zlib.crc32(name.encode()), seed]).standard_normal(out[name].shape)
        drawn = base * np.exp(spread * noise) if base else spread * noise
        out[name] = jnp.asarray(drawn.astype(out[name].dtype))
    for name, factor in factors.items():
        out[name] = (out[name] * factor).astype(out[name].dtype)
    return out
```

```python
from contextlib import ExitStack

import concourse.bass as bass
from concourse import mybir

F32 = mybir.dt.float32
F32R = mybir.dt.float32r
BF16 = mybir.dt.bfloat16
ACT = mybir.ActivationFunctionType
ALU = mybir.AluOpType
AX = mybir.AxisListType

P = 128
B, S, E = 8, 512, 128
NT = B * S // P
TB = S // P
NH, HD = 16, 64
HP = NH // 2
STEPS = B * HP
NX, I = 8, 512
IC = I // P
GATE_EPS, LN_EPS = 1e-6, 1e-5
MASKED = -1e30
UNITS = [(j, i) for i in (3, 0, 2, 1) for j in (0, 1)]
NU = len(UNITS)


def wait(engine, semaphore, value):
    if not isinstance(value, int) or value > 0:
        engine.wait_ge(semaphore, value)


def in_pairs(engine, count, body):
    body(0, 0)
    body(1, 1)
    with engine.Fori(1, count // 2) as i:
        body(2 * i, 0)
        body(2 * i + 1, 1)


def adaln_kernel(nc, x_in, w_qkv, w_out, gate_w, expert_bias, w_up, w_down, c_t, w_mod,
                 cos_in, sin_in, ident_in, mask_in, rank_in, out):
    ctx = ExitStack()
    with ctx:
        def sem(name):
            return ctx.enter_context(nc.semaphore(name))

        def sb(scope, name, shape, dt=F32):
            return scope.enter_context(nc.sbuf_tensor(name, shape, dt))

        ps = ctx.enter_context(nc.psum_tensor("ps", [P, 8, 512], F32))
        x_all = sb(ctx, "x_all", [P, NT, E])
        acc = sb(ctx, "acc", [P, NT, E])
        h_hi = sb(ctx, "h_hi", [P, NT * P], F32R)
        h_lo = sb(ctx, "h_lo", [P, NT * P], F32R)
        mod = sb(ctx, "mod", [P, B, 4, E])
        ident = sb(ctx, "ident", [P, P])
        gate_sb = sb(ctx, "gate_sb", [P, NX])
        bias_sb = sb(ctx, "bias_sb", [P, NX])
        rank = sb(ctx, "rank", [P, NX])
        logits = sb(ctx, "logits", [P, NT, NX])
        share = sb(ctx, "share", [P, NT, NX])
        stats = sb(ctx, "stats", [P, NT, 6])
        mean = sb(ctx, "mean", [P, NT])
        rstd = sb(ctx, "rstd", [P, NT])
        tmp = sb(ctx, "tmp", [P, 4, NT])

        def finish_stats(v, done, st, mean_, rstd_, root, t, n0, s_var, s_root):
            k = [n0]

            def step(ins):
                ins.then_inc(done, 1)
                k[0] = k[0] + 1
                wait(v, done, k[0])
            s0, s1, s2 = t
            step(v.tensor_tensor(s0, st[:, :, 1], st[:, :, 4], op=ALU.add))
            step(v.tensor_tensor(s1, st[:, :, 1], st[:, :, 4], op=ALU.subtract))
            step(v.tensor_scalar(mean_, s0, 0.5, None, ALU.mult))
            step(v.tensor_tensor(s1, s1, s1, op=ALU.mult))
            step(v.tensor_tensor(s2, st[:, :, 2], st[:, :, 5], op=ALU.add))
            step(v.tensor_scalar(s1, s1, 0.25, LN_EPS, ALU.mult, ALU.add))
            v.scalar_tensor_tensor(out=s1, in0=s2, scalar=1.0 / E, in1=s1, op0=ALU.mult,
                                   op1=ALU.add).then_inc(s_var, 1)
            return k, step

        def finish_root(v, step, root, rstd_, t):
            s0, s1, s2 = t
            step(v.reciprocal(rstd_, root))
            step(v.tensor_tensor(s0, rstd_, rstd_, op=ALU.mult))
            step(v.tensor_tensor(s0, s0, s1, op=ALU.mult))
            step(v.tensor_scalar(s0, s0, -0.5, 1.5, ALU.mult, ALU.add))
            step(v.tensor_tensor(rstd_, rstd_, s0, op=ALU.mult))

        att = ctx.enter_context(ExitStack())
        wq_hi = sb(att, "wq_hi", [P, HP * 384], F32R)
        wq_lo = sb(att, "wq_lo", [P, HP * 384], F32R)
        wo = sb(att, "wo", [P, HP * E])
        cos = sb(att, "cos", [P, TB, 256])
        sin = sb(att, "sin", [P, TB, 256])
        ident_b = sb(att, "ident_b", [P, P], BF16)
        mask_b = sb(att, "mask_b", [P, P], BF16)

        with ExitStack() as ph:
            wq_f = sb(ph, "wq_f", [P, HP * 384])
            mask_f = sb(ph, "mask_f", [P, P])
            mod1 = sb(ph, "mod1", [P, B, 2, E])
            ct = sb(ph, "ct", [P, 3, B])
            crep = sb(ph, "crep", [P, B, P])
            wm = sb(ph, "wm", [P, 6 * E])
            gt = sb(ph, "gt", [P, 2, B, E])
            xh = sb(ph, "xh1", [P, 2, TB, E])
            hn = sb(ph, "hn1", [P, 2, TB, E])
            d_x, d_w, d_c, d_k, s_rep, s_c, s_mm, s_mod, s_mod2, s_st, s_dve, s_var, s_root = (
                sem("a_" + n) for n in ("d_x", "d_w", "d_c", "d_k", "rep", "c", "mm", "mod", "mod2", "st",
                                        "dve", "var", "root"))
            s_xh, s_mul, s_hn, s_tr, s_hi, s_lo, s_whi, s_wlo, s_zero, s_sq, s_mr = (
                sem("a_" + n) for n in ("xh", "mul", "hn", "tr", "hi", "lo", "whi", "wlo", "zero", "sq", "mr"))
            with nc.Block() as block:
                @block.sync
                def _(e):
                    e.dma_start(ct[:, 0, :], c_t).then_inc(d_c, 16)
                    e.dma_start(wm[:], w_mod).then_inc(d_c, 16)
                    xv = x_in.rearrange("(n p) f -> p n f", p=P)
                    for q in range(4):
                        e.dma_start(x_all[:, 8 * q:8 * q + 8, :], xv[:, 8 * q:8 * q + 8, :]).then_inc(d_x, 16)
                        wait(e, d_x, 16 * q + 16)

                @block.gpsimd
                def _(e):
                    e.memset(acc[:], 0.0).then_inc(s_zero, 1)
                    wait(e, s_mod, 4)
                    def batch(b, par):
                        wait(e, s_xh, b + 1)
                        e.tensor_tensor(xh[:, par], xh[:, par],
                                        mod1[:, bass.ds(b, 1), 1:2, :].rearrange("p a c f -> p (a c) f")
                                        .to_broadcast([P, TB, E]), op=ALU.mult).then_inc(s_mul, 1)
                        wait(e, s_mul, b + 1)
                        wait(e, s_tr, b - 1)
                        e.tensor_tensor(hn[:, par], xh[:, par],
                                        mod1[:, bass.ds(b, 1), 0:1, :].rearrange("p a c f -> p (a c) f")
                                        .to_broadcast([P, TB, E]), op=ALU.add).then_inc(s_hn, 1)
                    in_pairs(e, B, batch)
                    wait(e, s_whi, 1)
                    e.tensor_tensor(wq_lo[:], wq_f[:], wq_hi[:], op=ALU.subtract).then_inc(s_wlo, 1)

                @block.scalar
                def _(e):
                    e.dma_start(wq_f[:], w_qkv).then_inc(d_w, 16)
                    e.dma_start(ident[:], ident_in).then_inc(d_k, 16)
                    e.dma_start(mask_f[:], mask_in).then_inc(d_k, 16)
                    e.dma_start(cos[:].rearrange("p t f -> p (t f)"), cos_in).then_inc(d_k, 16)
                    e.dma_start(sin[:].rearrange("p t f -> p (t f)"), sin_in).then_inc(d_k, 16)
                    e.dma_start(wo[:].rearrange("p (h f) -> p h f", h=HP),
                                w_out.rearrange("(h p) f -> p h f", p=P)).then_inc(d_k, 16)
                    e.dma_start(gate_sb[:], gate_w).then_inc(d_k, 16)
                    e.dma_start(rank[:], rank_in).then_inc(d_k, 16)
                    e.dma_start(bias_sb[:], expert_bias.partition_broadcast(P)).then_inc(d_k, 16)
                    wait(e, d_c, 32)
                    e.activation(ct[:, 1, :], ct[:, 0, :], ACT.Exp, scale=-1.0).then_inc(s_c, 1)
                    wait(e, d_w, 16)
                    e.copy(wq_hi[:], wq_f[:]).then_inc(s_whi, 1)
                    wait(e, s_var, 1)
                    e.activation(tmp[:, 3, :], tmp[:, 1, :], ACT.Sqrt).then_inc(s_root, 1)
                    def batch(b, par):
                        wait(e, s_tr, b + 1)
                        e.copy(h_hi[:, bass.ds(b * S, S)], ps[:, par, :]).then_inc(s_hi, 1)
                    in_pairs(e, B, batch)

                @block.tensor
                def _(e):
                    wait(e, s_rep, 1)
                    for b in range(B):
                        mm = e.matmul(ps[:, b, :], crep[:, b, :], wm[:, 0:512], start=True, stop=True)
                        mm.then_inc(s_mm, 1)
                    for b in range(B):
                        wait(e, s_mod2, 1 if b < B // 2 else 2)
                        mm = e.matmul(ps[:, b, 0:256], crep[:, b, :], wm[:, 512:768], start=True, stop=True)
                        mm.then_inc(s_mm, 1)
                    wait(e, d_k, 16 * 8)
                    wait(e, s_mod, 6)
                    def batch(b, par):
                        wait(e, s_hn, b + 1)
                        wait(e, s_lo, b - 1)
                        for t in range(TB):
                            mm = e.transpose(ps[:, par, t * P:(t + 1) * P], hn[:, par, t, :], ident[:])
                        mm.then_inc(s_tr, 1)
                    in_pairs(e, B, batch)

                @block.vector
                def _(e):
                    k = [0]

                    def step(ins):
                        ins.then_inc(s_dve, 1)
                        k[0] += 1
                        wait(e, s_dve, k[0])
                    wait(e, s_c, 1)
                    step(e.tensor_scalar(ct[:, 1, :], ct[:, 1, :], 1.0, None, ALU.add))
                    step(e.reciprocal(ct[:, 2, :], ct[:, 1, :]))
                    step(e.tensor_tensor(ct[:, 1, :], ct[:, 0, :], ct[:, 2, :], op=ALU.mult))
                    e.tensor_copy(crep[:], ct[:, 1, :].unsqueeze(2).to_broadcast([P, B, P])).then_inc(s_rep, 1)
                    wait(e, d_x, 64)
                    for n in range(NT):
                        e.bn_stats(stats[:, n, :], x_all[:, n, :]).then_inc(s_st, 1)
                    wait(e, s_st, NT)
                    t3 = (tmp[:, 0, :], tmp[:, 1, :], tmp[:, 2, :])
                    finish_stats(e, s_dve, stats, mean[:], rstd[:], None, t3, k[0], s_var, s_root)
                    k[0] += 6
                    wait(e, s_mm, B)
                    for half in range(2):
                        b0 = half * B // 2
                        src = ps[:, b0:b0 + B // 2, :].rearrange("p b (k f) -> p b k f", k=4)
                        e.tensor_copy(mod1[:, b0:b0 + B // 2, 0, :], src[:, :, 0, :]).then_inc(s_mod, 1)
                        e.tensor_scalar(mod1[:, b0:b0 + B // 2, 1, :], src[:, :, 1, :], 1.0, None,
                                        ALU.add).then_inc(s_mod, 1)
                        step(e.tensor_copy(mod[:, b0:b0 + B // 2, 0, :], src[:, :, 2, :]))
                        e.tensor_copy(mod[:, b0:b0 + B // 2, 1, :], src[:, :, 3, :]).then_inc(s_mod2, 1)
                    wait(e, s_mm, 2 * B)
                    src = ps[:, :, :].rearrange("p b (k f) -> p b k f", k=4)
                    e.tensor_scalar(mod[:, :, 2, :], src[:, :, 0, :], 1.0, None, ALU.add).then_inc(s_mod, 1)
                    e.tensor_copy(mod[:, :, 3, :], src[:, :, 1, :]).then_inc(s_mod, 1)
                    wait(e, s_root, 1)
                    finish_root(e, step, tmp[:, 3, :], rstd[:], t3)
                    def batch(b, par):
                        wait(e, s_hn, b - 1)
                        for t in range(TB):
                            ts = e.tensor_scalar(xh[:, par, t, :],
                                                 x_all[:, bass.ds(b * TB + t, 1), :].rearrange("p a f -> p (a f)"),
                                                 mean[:, bass.ds(b * TB + t, 1)], rstd[:, bass.ds(b * TB + t, 1)],
                                                 ALU.subtract, ALU.mult)
                        ts.then_inc(s_xh, 1)
                        wait(e, s_hi, b + 1)
                        e.tensor_tensor(h_lo[:, bass.ds(b * S, S)], ps[:, par, :], h_hi[:, bass.ds(b * S, S)],
                                        op=ALU.subtract).then_inc(s_lo, 1)
                    in_pairs(e, B, batch)
                    wait(e, s_mod, 6)
                    for g, m in enumerate((0, 3)):
                        src = mod[:, :, m, :]
                        step(e.tensor_scalar(gt[:, 0], src, 0.0, 2.0, ALU.is_ge, ALU.mult))
                        step(e.tensor_scalar(gt[:, 0], gt[:, 0], -1.0, None, ALU.add))
                        step(e.scalar_tensor_tensor(out=gt[:, 1], in0=src, scalar=-1.0, in1=src,
                                                    op0=ALU.mult, op1=ALU.max))
                        step(e.scalar_tensor_tensor(out=src, in0=gt[:, 1], scalar=0.25, in1=gt[:, 0],
                                                    op0=ALU.max, op1=ALU.mult))
                    wait(e, d_k, 16 * 8)
                    step(e.tensor_copy(ident_b[:], ident[:]))
                    step(e.tensor_copy(mask_b[:], mask_f[:]))

        with ExitStack() as ph:
            hb = [[sb(ph, f"hb{p}{q}", [P, S], F32R) for q in "hl"] for p in range(2)]
            raw = sb(ph, "raw", [P, TB, 256])
            rot = sb(ph, "rot", [P, TB, 256])
            qk = sb(ph, "qk", [P, TB, 256])
            v = [sb(ph, f"v{p}", [P, TB, 2 * HD]) for p in range(2)]
            qt = [[sb(ph, f"qt{p}{q}", [P, S], F32R) for q in "hl"] for p in range(2)]
            kt = [[sb(ph, f"kt{p}{q}", [P, S], F32R) for q in "hl"] for p in range(2)]
            prob = sb(ph, "prob", [P, 4, S])
            probt = [sb(ph, f"probt{p}", [P, 2, TB, S]) for p in range(2)]
            nmax = sb(ph, "nmax", [P, 2, NU])
            den = sb(ph, "den", [P, 2, NU])
            rden = sb(ph, "rden", [P, NU])
            rrep = sb(ph, "rrep", [P, TB, 2, HD])
            ones = sb(ph, "ones", [P, NU])
            rdt = sb(ph, "rdt", [P, S])
            ot = sb(ph, "ot", [P, S])
            (s_hb, p_prj, p_v, p_tr, p_s, p_pt, p_o, p_r, p_out, a_raw, a_v, a_hi, a_exp, a_pt, a_r,
             v_max, v_pt, v_cos, v_lo, v_rden, v_ot, v_acc, g_sin, g_rot, g_rep, g_one) = (
                sem("b_" + n) for n in (
                    "hb", "prj", "v", "tr", "s", "pt", "o", "r", "out", "araw", "av", "ahi", "aexp", "apt",
                    "ar", "vmax", "vpt", "vcos", "vlo", "vrden", "vot", "vacc", "gsin", "grot", "grep", "gone"))
            bank_s, bank_pt, bank_o, bank_r = 2, 4, 6, 7

            def width(u):
                return (UNITS[u][1] + 1) * P

            def work_bank(k, par):
                return ps[:, (k + par) % 2, :]

            def pe_project(e, n, par, t):
                nxt = 1 - par
                if t == 0:
                    wait(e, s_hb, 32 * (n + 2))
                if t < 2:
                    wait(e, v_lo, 2 * n + 1 + t)
                else:
                    wait(e, a_raw, 4 * (n + 1) + t - 1)
                o = work_bank(t, par)[:, 0:256]
                wc = ((n + 1) % HP) * 384
                hi, lo = (hb[nxt][q][:, t * P:(t + 1) * P] for q in range(2))
                e.matmul(o, hi, wq_hi[:, bass.ds(wc, 256)], start=True, stop=False)
                e.matmul(o, lo, wq_hi[:, bass.ds(wc, 256)], start=False, stop=False)
                e.matmul(o, hi, wq_lo[:, bass.ds(wc, 256)], start=False, stop=True).then_inc(p_prj, 1)

            def pe_v(e, n, par, last):
                if not last:
                    wait(e, a_raw, 4 * (n + 1) + 3)
                wc = (n % HP) * 384 + 256
                for t in range(TB):
                    o = work_bank(4, par)[:, t * P:(t + 1) * P]
                    hi, lo = (hb[par][q][:, t * P:(t + 1) * P] for q in range(2))
                    e.matmul(o, hi, wq_hi[:, bass.ds(wc, 128)], start=True, stop=False)
                    e.matmul(o, lo, wq_hi[:, bass.ds(wc, 128)], start=False, stop=False)
                    mm = e.matmul(o, hi, wq_lo[:, bass.ds(wc, 128)], start=False, stop=True)
                mm.then_inc(p_v, 1)

            def pe_turn(e, n, par, which):
                if which == 0:
                    wait(e, a_raw, 4 * (n + 1) + 4)
                    wait(e, g_rot, 2 * (n + 2))
                else:
                    wait(e, a_v, n + 1)
                for t in range(TB):
                    mm = e.transpose(work_bank(5 + which, par)[:, t * P:(t + 1) * P],
                                     qk[:, t, which * P:(which + 1) * P], ident[:])
                mm.then_inc(p_tr, 1)

            def pe_scores(e, n, par, u):
                g = NU * n + u
                if u == 0:
                    wait(e, v_lo, 2 * n + 2)
                wait(e, a_exp, g - 1)
                j, i = UNITS[u]
                w = width(u)
                o = ps[:, bank_s + u % 2, 0:w]
                rows = slice(j * HD, (j + 1) * HD)
                cols = slice(i * P, (i + 1) * P)
                e.matmul(o, qt[par][0][rows, cols], kt[par][0][rows, 0:w], start=True, stop=False)
                e.matmul(o, qt[par][1][rows, cols], kt[par][0][rows, 0:w], start=False, stop=False)
                e.matmul(o, qt[par][0][rows, cols], kt[par][1][rows, 0:w], start=False, stop=False)
                e.matmul(ps[:, bank_s + u % 2, w - P:w], ident_b[:], mask_b[:], start=False,
                         stop=True).then_inc(p_s, 1)

            def pe_turn_prob(e, n, u):
                g = NU * n + u
                wait(e, a_exp, g + 1)
                wait(e, a_pt if u % 2 else v_pt, 4 * n + u // 2)
                for kk in range(UNITS[u][1] + 1):
                    mm = e.transpose(ps[:, bank_pt + u % 2, kk * P:(kk + 1) * P],
                                     prob[:, u % 4, kk * P:(kk + 1) * P], ident[:])
                mm.then_inc(p_pt, 1)

            def pe_values(e, n, par):
                wait(e, v_pt, 4 * n + 4)
                wait(e, a_pt, 4 * n + 4)
                wait(e, a_v, n + 1)
                wait(e, v_ot, n)
                for kk in range(TB):
                    for j in range(2):
                        mm = e.matmul(ps[j * HD:(j + 1) * HD, bank_o, kk * P:S], v[par][:, kk, j * HD:(j + 1) * HD],
                                      probt[par][:, j, kk, kk * P:S], start=(kk == 0), stop=(kk == TB - 1))
                mm.then_inc(p_o, 1)
                wait(e, g_rep, n + 1)
                wait(e, v_acc, n)
                for i in range(TB):
                    mm = e.transpose(ps[:, bank_r, i * P:(i + 1) * P],
                                     rrep[:, i, :, :].rearrange("p j f -> p (j f)"), ident[:])
                mm.then_inc(p_r, 1)

            def pe_out(e, n):
                wait(e, v_ot, n + 1)
                for t in range(TB):
                    mm = e.matmul(ps[:, bank_r, t * P:(t + 1) * P], ot[:, t * P:(t + 1) * P],
                                  wo[:, bass.ds((n % HP) * E, E)], start=True, stop=True)
                mm.then_inc(p_out, 1)

            def pe_step(e, n, par, now=True, before=True, after=True):
                for u in range(NU):
                    if now:
                        pe_scores(e, n, par, u)
                    if u >= 2:
                        if now:
                            pe_turn_prob(e, n, u - 2)
                    elif before:
                        pe_turn_prob(e, n - 1, NU - 2 + u)
                    if after and u in (0, 1):
                        pe_project(e, n, par, 2 * u)
                        pe_project(e, n, par, 2 * u + 1)
                    if now and u == 2:
                        pe_v(e, n, par, not after)
                    if before and u == 3:
                        pe_values(e, n - 1, 1 - par)
                    if after and u == 5:
                        pe_turn(e, n, par, 0)
                        pe_turn(e, n, par, 1)
                    if before and u == 6:
                        pe_out(e, n - 1)

            def act_raw(e, n, par, t):
                m = n + 1
                wait(e, p_prj, 4 * m + t + 1)
                wait(e, v_cos, 2 * n + t // 2 + 1)
                wait(e, g_sin, 4 * n + 2 * (t // 2) + 2)
                e.copy(raw[:, t, :], work_bank(t, par)[:, 0:256]).then_inc(a_raw, 1)

            def act_v(e, n, par):
                wait(e, p_v, n + 1)
                wait(e, p_o, n - 1)
                e.copy(v[par][:].rearrange("p t f -> p (t f)"), work_bank(4, par)).then_inc(a_v, 1)

            def act_hi(e, n, par, which):
                wait(e, p_tr, 2 * (n + 1) + which + 1)
                wait(e, p_s, NU * n)
                dst = (qt, kt)[which][1 - par][0]
                e.copy(dst[:], work_bank(5 + which, par)).then_inc(a_hi, 1)

            def act_exp(e, n, par, u):
                g = NU * n + u
                j, i = UNITS[u]
                wait(e, v_max, g + 1)
                wait(e, p_pt, g - 3)
                if u == 0:
                    wait(e, v_rden, n - 1)
                e.activation(prob[:, u % 4, 0:width(u)], ps[:, bank_s + u % 2, 0:width(u)], ACT.Exp,
                             bias=nmax[:, par, u:u + 1],
                             accum_out=den[:, par, 2 * i + j:2 * i + j + 1]).then_inc(a_exp, 1)

            def store_prob(e, n, par, u, copy, done):
                j, i = UNITS[u]
                wait(e, p_pt, NU * n + u + 1)
                if u < 2:
                    wait(e, p_o, n - 1)
                copy(probt[par][:, j, 0:i + 1, i * P:(i + 1) * P],
                     ps[:, bank_pt + u % 2, 0:width(u)].rearrange("p (k q) -> p k q", q=P)).then_inc(done, 1)

            def act_r(e, n):
                wait(e, p_r, n + 1)
                wait(e, v_ot, n)
                e.copy(rdt[:], ps[:, bank_r, :]).then_inc(a_r, 1)

            def act_step(e, n, par, now=True, before=True, after=True):
                for u in range(NU):
                    if now:
                        act_exp(e, n, par, u)
                    if u >= 2:
                        if now and u % 2:
                            store_prob(e, n, par, u - 2, e.copy, a_pt)
                    elif before and u % 2:
                        store_prob(e, n - 1, 1 - par, NU - 2 + u, e.copy, a_pt)
                    if after and u in (0, 1):
                        act_raw(e, n, par, 2 * u)
                        act_raw(e, n, par, 2 * u + 1)
                    if now and u == 2:
                        act_v(e, n, par)
                    if before and u == 4:
                        act_r(e, n - 1)
                    if after and u == 5:
                        act_hi(e, n, par, 0)
                        act_hi(e, n, par, 1)

            def dve_max(e, n, par, u):
                g = NU * n + u
                wait(e, p_s, g + 1)
                e.tensor_reduce(nmax[:, par, u:u + 1], ps[:, bank_s + u % 2, 0:width(u)], AX.X, ALU.max,
                                negate=True).then_inc(v_max, 1)

            def dve_cos(e, n, half):
                m = n + 1
                wait(e, a_raw, 4 * m + 2 * half + 2)
                wait(e, p_tr, 2 * m)
                t = slice(2 * half, 2 * half + 2)
                e.tensor_tensor(qk[:, t, :], raw[:, t, :], cos[:, t, :], op=ALU.mult).then_inc(v_cos, 1)

            def dve_lo(e, n, par, which):
                wait(e, a_hi, 2 * (n + 1) + which + 1)
                hi, lo = (qt, kt)[which][1 - par]
                e.tensor_tensor(lo[:], work_bank(5 + which, par), hi[:], op=ALU.subtract).then_inc(v_lo, 1)

            def dve_rden(e, n, par):
                wait(e, a_exp, NU * (n + 1))
                wait(e, g_rep, n)
                e.reciprocal(rden[:], den[:, par, :]).then_inc(v_rden, 1)

            def dve_ot(e, n):
                wait(e, a_r, n + 1)
                wait(e, p_o, n + 1)
                wait(e, p_out, n)
                e.tensor_tensor(ot[:], ps[:, bank_o, :], rdt[:], op=ALU.mult).then_inc(v_ot, 1)

            def dve_acc(e, n):
                wait(e, p_out, n + 1)
                wait(e, v_acc, n)
                dst = acc[:, bass.ds((n // HP) * TB, TB), :]
                e.tensor_tensor(dst, ps[:, bank_r, :].rearrange("p (t f) -> p t f", t=TB), dst,
                                op=ALU.add).then_inc(v_acc, 1)

            def dve_step(e, n, par, now=True, before=True, after=True):
                for u in range(NU):
                    if now:
                        dve_max(e, n, par, u)
                    if before and u == 0:
                        dve_rden(e, n - 1, 1 - par)
                    if u >= 2:
                        if now and u % 2 == 0:
                            store_prob(e, n, par, u - 2, e.tensor_copy, v_pt)
                    elif before and u % 2 == 0:
                        store_prob(e, n - 1, 1 - par, NU - 2 + u, e.tensor_copy, v_pt)
                    if after and u in (1, 2):
                        dve_cos(e, n, u - 1)
                    if before and u == 5:
                        dve_ot(e, n - 1)
                    if after and u in (6, 7):
                        dve_lo(e, n, par, u - 6)
                    if before and u == 7:
                        dve_acc(e, n - 1)

            def pool_step(e, n, par, now=True, before=True, after=True):
                if before:
                    wait(e, v_rden, n)
                    wait(e, p_r, n - 1)
                    wide = rden[:].unsqueeze(2).to_broadcast([P, NU, HD])
                    e.tensor_tensor(rrep[:].rearrange("p t j f -> p (t j) f"), wide,
                                    ones[:].unsqueeze(2).to_broadcast([P, NU, HD]), op=ALU.mult).then_inc(g_rep, 1)
                if not after:
                    return
                m = n + 1
                for half in range(2):
                    t = slice(2 * half, 2 * half + 2)

                    def part(x, k):
                        return x[:, t, :].rearrange("p t (h k f) -> p (t h) k f", k=2, f=HD // 2)[:, :, k, :]
                    wait(e, a_raw, 4 * m + 2 * half + 2)
                    wait(e, g_rot, 2 * n + half + 1)
                    for k in range(2):
                        e.tensor_tensor(part(rot, k), part(raw, 1 - k), part(sin, k), op=ALU.mult).then_inc(g_sin, 1)
                    wait(e, v_cos, 2 * m + half + 1)
                    wait(e, g_sin, 4 * m + 2 * half + 2)
                    e.tensor_tensor(qk[:, t, :], qk[:, t, :], rot[:, t, :], op=ALU.add).then_inc(g_rot, 1)

            def all_steps(e, step):
                step(e, -1, 1, now=False, before=False)
                step(e, 0, 0, before=False)
                with e.Fori(0, (STEPS - 2) // 2) as i:
                    step(e, 2 * i + 1, 1)
                    step(e, 2 * i + 2, 0)
                step(e, STEPS - 1, 1, after=False)
                step(e, STEPS, 0, now=False, after=False)

            with nc.Block() as block:
                @block.sync
                def _(e):
                    def load(m, par):
                        cols = bass.ds(e.snap((m // HP) * S) if not isinstance(m, int) else (m // HP) * S, S)
                        if isinstance(m, int):
                            wait(e, s_hb, 32 * m)
                        wait(e, p_v, m - 1)
                        for q, src in enumerate((h_hi, h_lo)):
                            e.dma_start(hb[par][q][:].bitcast(F32), src[:, cols].bitcast(F32)).then_inc(s_hb, 16)
                    in_pairs(e, STEPS, load)

                @block.tensor
                def _(e):
                    all_steps(e, pe_step)

                @block.scalar
                def _(e):
                    all_steps(e, act_step)

                @block.vector
                def _(e):
                    all_steps(e, dve_step)

                @block.gpsimd
                def _(e):
                    e.memset(ones[:], 1.0).then_inc(g_one, 1)
                    wait(e, g_one, 1)
                    all_steps(e, pool_step)
        att.close()

        ffn = ctx.enter_context(ExitStack())
        h2 = sb(ffn, "h2", [P, NT, E])
        wu = [sb(ffn, f"wu{q}", [P, NX * I], F32R) for q in "hl"]
        wd = [sb(ffn, f"wd{q}", [P, NX * IC * E], F32R) for q in "hl"]
        with ExitStack() as ph:
            WH = NX * I // 2
            wtmp = sb(ph, "wtmp", [P, 2, WH])
            xh = sb(ph, "xh3", [P, 2, TB, E])
            hn = sb(ph, "hn3", [P, 2, TB, E])
            ht = sb(ph, "ht3", [P, 2, S])
            t1 = sb(ph, "t1", [P, 2, TB, E])
            r8 = sb(ph, "r8", [P, 4, NT, NX])
            r1 = sb(ph, "r1", [P, 4, NT])
            (d_w, s_t1, s_x1, s_st, s_dve, s_var, s_root, s_xh, s_mul, s_hn, s_keep, s_tr, s_ht, s_hi, s_lo,
             s_lg, s_lgs, s_whi, s_wlo, s_e) = (
                sem("c_" + n) for n in ("dw", "t1", "x1", "st", "dve", "var", "root", "xh", "mul", "hn", "keep",
                                        "tr", "ht", "hi", "lo", "lg", "lgs", "whi", "wlo", "e"))
            with nc.Block() as block:
                @block.sync
                def _(e):
                    for q in range(4):
                        wait(e, d_w, 16 * q)
                        wait(e, s_wlo, q - 1)
                        e.dma_start(wtmp[:, q % 2, :], (w_up, w_down)[q // 2][:, q % 2 * WH:(q % 2 + 1) * WH])\
                            .then_inc(d_w, 16)

                @block.gpsimd
                def _(e):
                    for q in range(4):
                        wait(e, s_whi, q + 1)
                        cols = slice(q % 2 * WH, (q % 2 + 1) * WH)
                        e.tensor_tensor((wu, wd)[q // 2][1][:, cols], wtmp[:, q % 2, :],
                                        (wu, wd)[q // 2][0][:, cols], op=ALU.subtract).then_inc(s_wlo, 1)

                    def batch(b, par):
                        rows = bass.ds(b * TB, TB)
                        wait(e, s_x1, b - 1)
                        e.tensor_tensor(t1[:, par], acc[:, rows, :],
                                        mod[:, bass.ds(b, 1), 0:1, :].rearrange("p a c f -> p (a c) f")
                                        .to_broadcast([P, TB, E]), op=ALU.mult).then_inc(s_t1, 1)
                    in_pairs(e, B, batch)
                    def batch(b, par):
                        wait(e, s_xh, b + 1)
                        e.tensor_tensor(xh[:, par], xh[:, par],
                                        mod[:, bass.ds(b, 1), 2:3, :].rearrange("p a c f -> p (a c) f")
                                        .to_broadcast([P, TB, E]), op=ALU.mult).then_inc(s_mul, 1)
                        wait(e, s_mul, b + 1)
                        wait(e, s_tr, b - 1)
                        wait(e, s_keep, b - 1)
                        e.tensor_tensor(hn[:, par], xh[:, par],
                                        mod[:, bass.ds(b, 1), 1:2, :].rearrange("p a c f -> p (a c) f")
                                        .to_broadcast([P, TB, E]), op=ALU.add).then_inc(s_hn, 1)
                    in_pairs(e, B, batch)

                @block.scalar
                def _(e):
                    for q in range(4):
                        wait(e, d_w, 16 * (q + 1))
                        e.copy((wu, wd)[q // 2][0][:, q % 2 * WH:(q % 2 + 1) * WH], wtmp[:, q % 2, :]).then_inc(s_whi, 1)
                    wait(e, s_var, 1)
                    e.activation(tmp[:, 3, :], tmp[:, 1, :], ACT.Sqrt).then_inc(s_root, 1)
                    def batch(b, par):
                        wait(e, s_hn, b + 1)
                        e.copy(h2[:, bass.ds(b * TB, TB), :], hn[:, par]).then_inc(s_keep, 1)
                        wait(e, s_tr, b + 1)
                        wait(e, s_lo, b - 1)
                        wait(e, s_lg, b - 1)
                        e.copy(ht[:, par, :], ps[:, par, :]).then_inc(s_ht, 1)
                    in_pairs(e, B, batch)
                    wait(e, s_dve, 12)
                    e.activation(r8[:, 1].rearrange("p n x -> p (n x)"), r8[:, 0].rearrange("p n x -> p (n x)"),
                                 ACT.Exp).then_inc(s_e, 1)

                @block.tensor
                def _(e):
                    def batch(b, par):
                        wait(e, s_hn, b + 1)
                        wait(e, s_ht, b - 1)
                        for t in range(TB):
                            mm = e.transpose(ps[:, par, t * P:(t + 1) * P], hn[:, par, t, :], ident[:])
                        mm.then_inc(s_tr, 1)
                        wait(e, s_ht, b + 1)
                        wait(e, s_lgs, b - 1)
                        for t in range(TB):
                            mm = e.matmul(ps[:, 2 + par, t * NX:(t + 1) * NX], ht[:, par, t * P:(t + 1) * P],
                                          gate_sb[:], start=True, stop=True)
                        mm.then_inc(s_lg, 1)
                    in_pairs(e, B, batch)

                @block.vector
                def _(e):
                    k = [0]

                    def step(ins):
                        ins.then_inc(s_dve, 1)
                        k[0] += 1
                        wait(e, s_dve, k[0])
                    def batch(b, par):
                        rows = bass.ds(b * TB, TB)
                        wait(e, s_t1, b + 1)
                        e.tensor_tensor(x_all[:, rows, :], x_all[:, rows, :], t1[:, par],
                                        op=ALU.add).then_inc(s_x1, 1)
                    in_pairs(e, B, batch)
                    wait(e, s_x1, B)

                    def batch(b, par):
                        for t in range(TB):
                            e.bn_stats(stats[:, bass.ds(b * TB + t, 1), :].rearrange("p a f -> p (a f)"),
                                       x_all[:, bass.ds(b * TB + t, 1), :].rearrange("p a f -> p (a f)"))\
                                .then_inc(s_st, 1)
                    in_pairs(e, B, batch)
                    wait(e, s_st, NT)
                    t3 = (tmp[:, 0, :], tmp[:, 1, :], tmp[:, 2, :])
                    finish_stats(e, s_dve, stats, mean[:], rstd[:], None, t3, 0, s_var, s_root)
                    k[0] = 6
                    wait(e, s_root, 1)
                    finish_root(e, step, tmp[:, 3, :], rstd[:], t3)
                    def batch(b, par):
                        wait(e, s_hn, b - 1)
                        for t in range(TB):
                            ts = e.tensor_scalar(xh[:, par, t, :],
                                                 x_all[:, bass.ds(b * TB + t, 1), :].rearrange("p a f -> p (a f)"),
                                                 mean[:, bass.ds(b * TB + t, 1)], rstd[:, bass.ds(b * TB + t, 1)],
                                                 ALU.subtract, ALU.mult)
                        ts.then_inc(s_xh, 1)
                        wait(e, s_ht, b + 1)
                        cols = bass.ds(b * S, S)
                        e.tensor_copy(h_hi[:, cols], ht[:, par, :]).then_inc(s_hi, 1)
                        wait(e, s_hi, b + 1)
                        e.tensor_tensor(h_lo[:, cols], ht[:, par, :], h_hi[:, cols],
                                        op=ALU.subtract).then_inc(s_lo, 1)
                        wait(e, s_lg, b + 1)
                        e.tensor_tensor(logits[:, bass.ds(b * TB, TB), :],
                                        ps[:, 2 + par, 0:TB * NX].rearrange("p (t x) -> p t x", x=NX),
                                        bias_sb[:].unsqueeze(1).to_broadcast([P, TB, NX]),
                                        op=ALU.add).then_inc(s_lgs, 1)
                    in_pairs(e, B, batch)
                    wait(e, s_lgs, B)

                    def over(a):
                        return a.unsqueeze(2).to_broadcast([P, NT, NX])
                    rk = rank[:].unsqueeze(1).to_broadcast([P, NT, NX])
                    top = r1[:, 0, :]
                    e.tensor_reduce(top, logits[:], AX.X, ALU.max).then_inc(s_lgs, 1)
                    wait(e, s_lgs, B + 1)
                    step(e.tensor_tensor(r8[:, 0], logits[:], over(top), op=ALU.subtract))
                    assert k[0] == 12
                    wait(e, s_e, 1)
                    step(e.tensor_reduce(r1[:, 1, :], r8[:, 1], AX.X, ALU.add))
                    step(e.reciprocal(r1[:, 2, :], r1[:, 1, :]))
                    step(e.tensor_tensor(r8[:, 1], r8[:, 1], over(r1[:, 2, :]), op=ALU.mult))
                    chosen = share[:]
                    for turn in range(2):
                        best = r1[:, turn, :]
                        step(e.tensor_reduce(best, r8[:, 1], AX.X, ALU.max))
                        step(e.tensor_tensor(r8[:, 2], r8[:, 1], over(best), op=ALU.is_equal))
                        step(e.tensor_tensor(r8[:, 2], r8[:, 2], rk, op=ALU.mult))
                        step(e.tensor_reduce(r1[:, 2, :], r8[:, 2], AX.X, ALU.max))
                        step(e.tensor_tensor(r8[:, 2], rk, over(r1[:, 2, :]), op=ALU.is_equal))
                        step(e.scalar_tensor_tensor(out=r8[:, 1], in0=r8[:, 2], scalar=-2.0, in1=r8[:, 1],
                                                    op0=ALU.mult, op1=ALU.add))
                        if turn == 0:
                            step(e.tensor_tensor(chosen, r8[:, 2], over(best), op=ALU.mult))
                        else:
                            step(e.tensor_tensor(r8[:, 3], r8[:, 2], over(best), op=ALU.mult))
                            step(e.tensor_tensor(chosen, chosen, r8[:, 3], op=ALU.add))
                    step(e.tensor_tensor(r1[:, 2, :], r1[:, 0, :], r1[:, 1, :], op=ALU.add))
                    step(e.tensor_scalar(r1[:, 2, :], r1[:, 2, :], GATE_EPS, None, ALU.add))
                    step(e.reciprocal(r1[:, 3, :], r1[:, 2, :]))
                    step(e.tensor_tensor(chosen, chosen, over(r1[:, 3, :]), op=ALU.mult))

        with ExitStack() as ph:
            NC = NX * IC
            hf = sb(ph, "hf", [P, 4, S])
            hh = sb(ph, "hh", [P, 4, S], F32R)
            hl = sb(ph, "hl", [P, 4, S], F32R)
            st4 = sb(ph, "st4", [P, TB, 6])
            m4 = sb(ph, "m4", [P, TB])
            r4 = sb(ph, "r4", [P, TB])
            t4 = sb(ph, "t4", [P, 4, TB])
            y4 = sb(ph, "y4", [P, TB, E])
            pause = sb(ph, "pause", [P, 1])
            (p_up, p_dn, a_ge, v_hi, v_lo, v_acc, v_st, v_var, a_root, v_y, g_y, d_out) = (
                sem("d_" + n) for n in ("up", "dn", "ge", "hi", "lo", "acc", "st", "var", "root", "y", "gy", "out"))
            LAG = 3
            bank_y = 4

            def up(e, n, k):
                g = NC * n + k
                wait(e, a_ge, g - 3)
                o = ps[:, k % 4, :]
                w = slice(k * P, (k + 1) * P)
                cols = bass.ds(n * S, S)
                e.matmul(o, wu[0][:, w], h_hi[:, cols], start=True, stop=False)
                e.matmul(o, wu[0][:, w], h_lo[:, cols], start=False, stop=False)
                e.matmul(o, wu[1][:, w], h_hi[:, cols], start=False, stop=True).then_inc(p_up, 1)

            def down(e, n, k):
                g = NC * n + k
                x, c = divmod(k, IC)
                wait(e, v_lo, g + 1)
                if c == 0:
                    wait(e, v_acc, NX * n + x - 1)
                w = slice(k * E, (k + 1) * E)
                for t in range(TB):
                    o = ps[:, bank_y + x % 2, t * P:(t + 1) * P]
                    cols = slice(t * P, (t + 1) * P)
                    e.matmul(o, hh[:, k % 4, cols], wd[0][:, w], start=(c == 0 and t == 0), stop=False,
                             skip_group_check=True)
                    e.matmul(o, hl[:, k % 4, cols], wd[0][:, w], start=False, stop=False, skip_group_check=True)
                    mm = e.matmul(o, hh[:, k % 4, cols], wd[1][:, w], start=False, stop=(c == IC - 1),
                                  skip_group_check=True)
                mm.then_inc(p_dn, 1)

            def pe4(e, n, now=True, before=True):
                for k in range(NC):
                    if now:
                        up(e, n, k)
                    if k >= LAG:
                        if now:
                            down(e, n, k - LAG)
                    elif before:
                        down(e, n - 1, NC - LAG + k)

            def act4(e, n, now=True, before=True):
                for k in range(NC):
                    if now:
                        g = NC * n + k
                        wait(e, p_up, g + 1)
                        wait(e, v_lo, g - 3)
                        e.activation(hf[:, k % 4, :], ps[:, k % 4, :], ACT.Gelu).then_inc(a_ge, 1)
                    if before and k == 9:
                        wait(e, v_var, n)
                        e.activation(t4[:, 3, :], t4[:, 1, :], ACT.Sqrt).then_inc(a_root, 1)

            def add_up(e, n, x):
                wait(e, p_dn, NC * n + IC * (x + 1))
                wait(e, v_acc, NX * n + x)
                for t in range(TB):
                    dst = acc[:, bass.ds(n * TB + t, 1), :].rearrange("p a f -> p (a f)")
                    src = ps[:, bank_y + x % 2, t * P:(t + 1) * P]
                    wt = share[:, bass.ds(n * TB + t, 1), x:x + 1].rearrange("p a f -> p (a f)")
                    if x == 0:
                        ins = e.tensor_scalar(dst, src, wt, None, ALU.mult)
                    else:
                        ins = e.scalar_tensor_tensor(out=dst, in0=src, scalar=wt, in1=dst, op0=ALU.mult, op1=ALU.add)
                ins.then_inc(v_acc, 1)

            NV = 6 + 5

            def dve4(e, n, now=True, before=True):
                for k in range(NC):
                    if now:
                        g = NC * n + k
                        wait(e, a_ge, g + 1)
                        wait(e, p_dn, g - 3)
                        e.tensor_copy(hh[:, k % 4, :], hf[:, k % 4, :]).then_inc(v_hi, 1)
                        wait(e, v_hi, g + 1)
                        e.tensor_tensor(hl[:, k % 4, :], hf[:, k % 4, :], hh[:, k % 4, :],
                                        op=ALU.subtract).then_inc(v_lo, 1)
                    q = k - LAG - 1
                    if q % IC == IC - 1:
                        if q >= 0 and now:
                            add_up(e, n, q // IC)
                        if q < 0 and before:
                            add_up(e, n - 1, NX - 1)
                    if before and k == 5:
                        m = n - 1
                        wait(e, v_acc, NX * n)
                        e.memset(pause[:], 0.0)
                        for t in range(TB):
                            e.bn_stats(st4[:, t, :], acc[:, bass.ds(m * TB + t, 1), :].rearrange("p a f -> p (a f)"))\
                                .then_inc(v_st, 1)
                        base = (TB + NV) * m + TB
                        wait(e, v_st, base)
                        t3 = (t4[:, 0, :], t4[:, 1, :], t4[:, 2, :])
                        finish_stats(e, v_st, st4, m4[:], r4[:], None, t3, base, v_var, a_root)
                    if before and k == 12:
                        m = n - 1
                        at = [(TB + NV) * m + TB + 6]

                        def step(ins):
                            ins.then_inc(v_st, 1)
                            at[0] = at[0] + 1
                            wait(e, v_st, at[0])
                        wait(e, a_root, n)
                        finish_root(e, step, t4[:, 3, :], r4[:], (t4[:, 0, :], t4[:, 1, :], t4[:, 2, :]))
                        wait(e, g_y, 3 * m)
                        for t in range(TB):
                            ts = e.tensor_scalar(y4[:, t, :], acc[:, bass.ds(m * TB + t, 1), :].rearrange("p a f -> p (a f)"),
                                                 m4[:, t:t + 1], r4[:, t:t + 1], ALU.subtract, ALU.mult)
                        ts.then_inc(v_y, 1)

            def pool4(e, m):
                rows = bass.ds(m * TB, TB)
                wait(e, v_y, m + 1)
                e.tensor_tensor(y4[:], y4[:], h2[:, rows, :], op=ALU.add).then_inc(g_y, 1)
                wait(e, g_y, 3 * m + 1)
                e.tensor_tensor(y4[:], y4[:], mod[:, bass.ds(m, 1), 3:4, :].rearrange("p a c f -> p (a c) f")
                                .to_broadcast([P, TB, E]), op=ALU.mult).then_inc(g_y, 1)
                wait(e, g_y, 3 * m + 2)
                e.tensor_tensor(x_all[:, rows, :], x_all[:, rows, :], y4[:], op=ALU.add).then_inc(g_y, 1)

            def all_batches(e, step):
                step(e, 0, before=False)
                with e.Fori(1, B) as n:
                    step(e, n)
                step(e, B, now=False)

            with nc.Block() as block:
                @block.tensor
                def _(e):
                    all_batches(e, pe4)

                @block.scalar
                def _(e):
                    all_batches(e, act4)

                @block.vector
                def _(e):
                    all_batches(e, dve4)

                @block.gpsimd
                def _(e):
                    with e.Fori(0, B) as m:
                        pool4(e, m)

                @block.sync
                def _(e):
                    ov = out.rearrange("(n p) f -> p n f", p=P)
                    with e.Fori(0, B) as m:
                        wait(e, g_y, 3 * m + 3)
                        e.dma_start(ov[:, bass.ds(m * TB, TB), :], x_all[:, bass.ds(m * TB, TB), :]).then_inc(d_out, 16)
                    wait(e, d_out, 16 * B)


def kernel(L0_attn_x, L0_attn_W_qkv, L0_attn_W_out, L0_ffn_gate_w, L0_ffn_expert_bias, L0_ffn_w_up, L0_ffn_w_down,
           L0_c, L0_wmod):
    import numpy as np
    import concourse.bacc as bacc
    from concourse.bass_utils import run_bass_kernel_spmd

    w = np.asarray(L0_attn_W_qkv).reshape(E, 3, HP, 2, HD)
    order = np.concatenate([np.arange(0, HD, 2), np.arange(1, HD, 2)])
    w = np.stack([w[:, 0][..., order], w[:, 1][..., order], w[:, 2]], axis=2)
    freqs = (1.0 / np.float32(10000.0) ** (np.arange(0, HD, 2) / HD).astype(np.float32)).astype(np.float32)
    angles = np.arange(S, dtype=np.float32)[:, None] * freqs[None, :]
    co, si = np.cos(angles), np.sin(angles)
    scale = np.repeat(np.array([HD ** -0.5, 1.0], np.float32), 2)[None, :, None]
    cos4 = np.concatenate([co, co], 1)[:, None, :] * scale
    sin4 = np.concatenate([-si, si], 1)[:, None, :] * scale

    def by_tile(a):
        return np.ascontiguousarray(a.reshape(TB, P, 256).transpose(1, 0, 2).reshape(P, TB * 256), np.float32)
    arrays = {
        "x": np.asarray(L0_attn_x).reshape(B * S, E),
        "w_qkv": np.ascontiguousarray(w.reshape(E, HP * 384)),
        "w_out": np.asarray(L0_attn_W_out),
        "gate_w": np.ascontiguousarray(np.asarray(L0_ffn_gate_w).T),
        "expert_bias": np.asarray(L0_ffn_expert_bias),
        "w_up": np.ascontiguousarray(np.asarray(L0_ffn_w_up).transpose(2, 0, 1).reshape(E, NX * I)),
        "w_down": np.ascontiguousarray(np.asarray(L0_ffn_w_down).reshape(NX, E, IC, P).transpose(3, 0, 2, 1)
                                       .reshape(P, NX * IC * E)),
        "c_t": np.ascontiguousarray(np.asarray(L0_c).T),
        "w_mod": np.asarray(L0_wmod),
        "cos": by_tile(cos4),
        "sin": by_tile(sin4),
        "ident": np.eye(P, dtype=np.float32),
        "mask": np.triu(np.full((P, P), MASKED, np.float32), 1),
        "rank": np.tile(np.arange(NX, 0, -1, dtype=np.float32), (P, 1)),
    }
    nc = bacc.Bacc("TRN2", target_bir_lowering=False, num_devices=1)
    args = [nc.dram_tensor("in_" + name, a.shape, mybir.dt.from_np(a.dtype), kind="ExternalInput").ap()
            for name, a in arrays.items()]
    args.append(nc.dram_tensor("out", (B * S, E), F32, kind="ExternalOutput").ap())
    adaln_kernel(nc, *args)
    r = run_bass_kernel_spmd(nc, [{"in_" + name: a for name, a in arrays.items()}], core_ids=[0])
    return r.results[0]["out"].reshape(B, S, E)
```

```python
from contextlib import ExitStack

import concourse.bass as bass
from concourse import mybir

F32 = mybir.dt.float32
F32R = mybir.dt.float32r
BF16 = mybir.dt.bfloat16
ACT = mybir.ActivationFunctionType
ALU = mybir.AluOpType
AX = mybir.AxisListType

P = 128
B, S, E = 8, 512, 128
NT = B * S // P
TB = S // P
NH, HD = 16, 64
HP = NH // 2
STEPS = B * HP
NX, I = 8, 512
IC = I // P
GATE_EPS, LN_EPS = 1e-6, 1e-5
MASKED = -1e30
UNITS = [(j, i) for i in (3, 0, 2, 1) for j in (0, 1)]
NU = len(UNITS)


def wait(engine, semaphore, value):
    if not isinstance(value, int) or value > 0:
        engine.wait_ge(semaphore, value)


def in_pairs(engine, count, body):
    body(0, 0)
    body(1, 1)
    with engine.Fori(1, count // 2) as i:
        body(2 * i, 0)
        body(2 * i + 1, 1)


def adaln_kernel(nc, x_in, w_qkv, w_out, gate_w, expert_bias, w_up, w_down, c_t, w_mod,
                 cos_in, sin_in, ident_in, mask_in, rank_in, out):
    ctx = ExitStack()
    with ctx:
        def sem(name):
            return ctx.enter_context(nc.semaphore(name))

        def sb(scope, name, shape, dt=F32):
            return scope.enter_context(nc.sbuf_tensor(name, shape, dt))

        ps = ctx.enter_context(nc.psum_tensor("ps", [P, 8, 512], F32))
        x_all = sb(ctx, "x_all", [P, NT, E])
        acc = sb(ctx, "acc", [P, NT, E])
        h_hi = sb(ctx, "h_hi", [P, NT * P], F32R)
        h_lo = sb(ctx, "h_lo", [P, NT * P], F32R)
        mod = sb(ctx, "mod", [P, B, 4, E])
        ident = sb(ctx, "ident", [P, P])
        gate_sb = sb(ctx, "gate_sb", [P, NX])
        bias_sb = sb(ctx, "bias_sb", [P, NX])
        rank = sb(ctx, "rank", [P, NX])
        stats = sb(ctx, "stats", [P, NT, 6])
        mean = sb(ctx, "mean", [P, NT])
        rstd = sb(ctx, "rstd", [P, NT])
        tmp = sb(ctx, "tmp", [P, 4, NT])

        def finish_stats(v, done, st, mean_, rstd_, root, t, n0, s_var, s_root):
            k = [n0]

            def step(ins):
                ins.then_inc(done, 1)
                k[0] = k[0] + 1
                wait(v, done, k[0])
            s0, s1, s2 = t
            step(v.tensor_tensor(s0, st[:, :, 1], st[:, :, 4], op=ALU.add))
            step(v.tensor_tensor(s1, st[:, :, 1], st[:, :, 4], op=ALU.subtract))
            step(v.tensor_scalar(mean_, s0, 0.5, None, ALU.mult))
            step(v.tensor_tensor(s1, s1, s1, op=ALU.mult))
            step(v.tensor_tensor(s2, st[:, :, 2], st[:, :, 5], op=ALU.add))
            step(v.tensor_scalar(s1, s1, 0.25, LN_EPS, ALU.mult, ALU.add))
            v.scalar_tensor_tensor(out=s1, in0=s2, scalar=1.0 / E, in1=s1, op0=ALU.mult,
                                   op1=ALU.add).then_inc(s_var, 1)
            return k, step

        def finish_root(v, step, root, rstd_, t):
            s0, s1, s2 = t
            step(v.reciprocal(rstd_, root))
            step(v.tensor_tensor(s0, rstd_, rstd_, op=ALU.mult))
            step(v.tensor_tensor(s0, s0, s1, op=ALU.mult))
            step(v.tensor_scalar(s0, s0, -0.5, 1.5, ALU.mult, ALU.add))
            step(v.tensor_tensor(rstd_, rstd_, s0, op=ALU.mult))

        att = ctx.enter_context(ExitStack())
        wq_hi = sb(att, "wq_hi", [P, HP * 384], F32R)
        wq_lo = sb(att, "wq_lo", [P, HP * 384], F32R)
        wo = sb(att, "wo", [P, HP * E])
        cos = sb(att, "cos", [P, TB, 256])
        sin = sb(att, "sin", [P, TB, 256])
        ident_b = sb(att, "ident_b", [P, P], BF16)
        mask_b = sb(att, "mask_b", [P, P], BF16)

        with ExitStack() as ph:
            wq_f = sb(ph, "wq_f", [P, HP * 384])
            mask_f = sb(ph, "mask_f", [P, P])
            mod1 = sb(ph, "mod1", [P, B, 2, E])
            ct = sb(ph, "ct", [P, 3, B])
            crep = sb(ph, "crep", [P, B, P])
            wm = sb(ph, "wm", [P, 6 * E])
            gt = sb(ph, "gt", [P, 2, B, E])
            xh = sb(ph, "xh1", [P, 2, TB, E])
            hn = sb(ph, "hn1", [P, 2, TB, E])
            d_x, d_w, d_c, d_k, s_rep, s_c, s_mm, s_mod, s_mod2, s_st, s_dve, s_var, s_root = (
                sem("a_" + n) for n in ("d_x", "d_w", "d_c", "d_k", "rep", "c", "mm", "mod", "mod2", "st",
                                        "dve", "var", "root"))
            s_xh, s_mul, s_hn, s_tr, s_hi, s_lo, s_whi, s_wlo, s_zero, s_sq, s_mr = (
                sem("a_" + n) for n in ("xh", "mul", "hn", "tr", "hi", "lo", "whi", "wlo", "zero", "sq", "mr"))
            with nc.Block() as block:
                @block.sync
                def _(e):
                    e.dma_start(ct[:, 0, :], c_t).then_inc(d_c, 16)
                    e.dma_start(wm[:], w_mod).then_inc(d_c, 16)
                    xv = x_in.rearrange("(n p) f -> p n f", p=P)
                    for q in range(4):
                        e.dma_start(x_all[:, 8 * q:8 * q + 8, :], xv[:, 8 * q:8 * q + 8, :]).then_inc(d_x, 16)
                        wait(e, d_x, 16 * q + 16)

                @block.gpsimd
                def _(e):
                    e.memset(acc[:], 0.0).then_inc(s_zero, 1)
                    wait(e, s_mod, 4)
                    def batch(b, par):
                        wait(e, s_xh, b + 1)
                        e.tensor_tensor(xh[:, par], xh[:, par],
                                        mod1[:, bass.ds(b, 1), 1:2, :].rearrange("p a c f -> p (a c) f")
                                        .to_broadcast([P, TB, E]), op=ALU.mult).then_inc(s_mul, 1)
                        wait(e, s_mul, b + 1)
                        wait(e, s_tr, b - 1)
                        e.tensor_tensor(hn[:, par], xh[:, par],
                                        mod1[:, bass.ds(b, 1), 0:1, :].rearrange("p a c f -> p (a c) f")
                                        .to_broadcast([P, TB, E]), op=ALU.add).then_inc(s_hn, 1)
                    in_pairs(e, B, batch)
                    wait(e, s_whi, 1)
                    e.tensor_tensor(wq_lo[:], wq_f[:], wq_hi[:], op=ALU.subtract).then_inc(s_wlo, 1)

                @block.scalar
                def _(e):
                    e.dma_start(wq_f[:], w_qkv).then_inc(d_w, 16)
                    e.dma_start(ident[:], ident_in).then_inc(d_k, 16)
                    e.dma_start(mask_f[:], mask_in).then_inc(d_k, 16)
                    e.dma_start(cos[:].rearrange("p t f -> p (t f)"), cos_in).then_inc(d_k, 16)
                    e.dma_start(sin[:].rearrange("p t f -> p (t f)"), sin_in).then_inc(d_k, 16)
                    e.dma_start(wo[:].rearrange("p (h f) -> p h f", h=HP),
                                w_out.rearrange("(h p) f -> p h f", p=P)).then_inc(d_k, 16)
                    e.dma_start(gate_sb[:], gate_w).then_inc(d_k, 16)
                    e.dma_start(rank[:], rank_in).then_inc(d_k, 16)
                    e.dma_start(bias_sb[:], expert_bias.partition_broadcast(P)).then_inc(d_k, 16)
                    wait(e, d_c, 32)
                    e.activation(ct[:, 1, :], ct[:, 0, :], ACT.Exp, scale=-1.0).then_inc(s_c, 1)
                    wait(e, d_w, 16)
                    e.copy(wq_hi[:], wq_f[:]).then_inc(s_whi, 1)
                    wait(e, s_var, 1)
                    e.activation(tmp[:, 3, :], tmp[:, 1, :], ACT.Sqrt).then_inc(s_root, 1)
                    def batch(b, par):
                        wait(e, s_tr, b + 1)
                        e.copy(h_hi[:, bass.ds(b * S, S)], ps[:, par, :]).then_inc(s_hi, 1)
                    in_pairs(e, B, batch)

                @block.tensor
                def _(e):
                    wait(e, s_rep, 1)
                    for b in range(B):
                        mm = e.matmul(ps[:, b, :], crep[:, b, :], wm[:, 0:512], start=True, stop=True)
                        mm.then_inc(s_mm, 1)
                    for b in range(B):
                        wait(e, s_mod2, 1 if b < B // 2 else 2)
                        mm = e.matmul(ps[:, b, 0:256], crep[:, b, :], wm[:, 512:768], start=True, stop=True)
                        mm.then_inc(s_mm, 1)
                    wait(e, d_k, 16 * 8)
                    wait(e, s_mod, 6)
                    def batch(b, par):
                        wait(e, s_hn, b + 1)
                        wait(e, s_lo, b - 1)
                        for t in range(TB):
                            mm = e.transpose(ps[:, par, t * P:(t + 1) * P], hn[:, par, t, :], ident[:])
                        mm.then_inc(s_tr, 1)
                    in_pairs(e, B, batch)

                @block.vector
                def _(e):
                    k = [0]

                    def step(ins):
                        ins.then_inc(s_dve, 1)
                        k[0] += 1
                        wait(e, s_dve, k[0])
                    wait(e, s_c, 1)
                    step(e.tensor_scalar(ct[:, 1, :], ct[:, 1, :], 1.0, None, ALU.add))
                    step(e.reciprocal(ct[:, 2, :], ct[:, 1, :]))
                    step(e.tensor_tensor(ct[:, 1, :], ct[:, 0, :], ct[:, 2, :], op=ALU.mult))
                    e.tensor_copy(crep[:], ct[:, 1, :].unsqueeze(2).to_broadcast([P, B, P])).then_inc(s_rep, 1)
                    wait(e, d_x, 64)
                    for n in range(NT):
                        e.bn_stats(stats[:, n, :], x_all[:, n, :]).then_inc(s_st, 1)
                    wait(e, s_st, NT)
                    t3 = (tmp[:, 0, :], tmp[:, 1, :], tmp[:, 2, :])
                    finish_stats(e, s_dve, stats, mean[:], rstd[:], None, t3, k[0], s_var, s_root)
                    k[0] += 6
                    wait(e, s_mm, B)
                    for half in range(2):
                        b0 = half * B // 2
                        src = ps[:, b0:b0 + B // 2, :].rearrange("p b (k f) -> p b k f", k=4)
                        e.tensor_copy(mod1[:, b0:b0 + B // 2, 0, :], src[:, :, 0, :]).then_inc(s_mod, 1)
                        e.tensor_scalar(mod1[:, b0:b0 + B // 2, 1, :], src[:, :, 1, :], 1.0, None,
                                        ALU.add).then_inc(s_mod, 1)
                        step(e.tensor_copy(mod[:, b0:b0 + B // 2, 0, :], src[:, :, 2, :]))
                        e.tensor_copy(mod[:, b0:b0 + B // 2, 1, :], src[:, :, 3, :]).then_inc(s_mod2, 1)
                    wait(e, s_mm, 2 * B)
                    src = ps[:, :, :].rearrange("p b (k f) -> p b k f", k=4)
                    e.tensor_scalar(mod[:, :, 2, :], src[:, :, 0, :], 1.0, None, ALU.add).then_inc(s_mod, 1)
                    e.tensor_copy(mod[:, :, 3, :], src[:, :, 1, :]).then_inc(s_mod, 1)
                    wait(e, s_root, 1)
                    finish_root(e, step, tmp[:, 3, :], rstd[:], t3)
                    def batch(b, par):
                        wait(e, s_hn, b - 1)
                        for t in range(TB):
                            ts = e.tensor_scalar(xh[:, par, t, :],
                                                 x_all[:, bass.ds(b * TB + t, 1), :].rearrange("p a f -> p (a f)"),
                                                 mean[:, bass.ds(b * TB + t, 1)], rstd[:, bass.ds(b * TB + t, 1)],
                                                 ALU.subtract, ALU.mult)
                        ts.then_inc(s_xh, 1)
                        wait(e, s_hi, b + 1)
                        e.tensor_tensor(h_lo[:, bass.ds(b * S, S)], ps[:, par, :], h_hi[:, bass.ds(b * S, S)],
                                        op=ALU.subtract).then_inc(s_lo, 1)
                    in_pairs(e, B, batch)
                    wait(e, s_mod, 6)
                    for g, m in enumerate((0, 3)):
                        src = mod[:, :, m, :]
                        step(e.tensor_scalar(gt[:, 0], src, 0.0, 2.0, ALU.is_ge, ALU.mult))
                        step(e.tensor_scalar(gt[:, 0], gt[:, 0], -1.0, None, ALU.add))
                        step(e.scalar_tensor_tensor(out=gt[:, 1], in0=src, scalar=-1.0, in1=src,
                                                    op0=ALU.mult, op1=ALU.max))
                        step(e.scalar_tensor_tensor(out=src, in0=gt[:, 1], scalar=0.25, in1=gt[:, 0],
                                                    op0=ALU.max, op1=ALU.mult))
                    wait(e, d_k, 16 * 8)
                    step(e.tensor_copy(ident_b[:], ident[:]))
                    step(e.tensor_copy(mask_b[:], mask_f[:]))

        with ExitStack() as ph:
            hb = [[sb(ph, f"hb{p}{q}", [P, S], F32R) for q in "hl"] for p in range(2)]
            raw = [sb(ph, f"raw{p}", [P, TB, 384]) for p in range(2)]
            rot = sb(ph, "rot", [P, TB, 256])
            qk = sb(ph, "qk", [P, TB, 256])
            qt = [[sb(ph, f"qt{p}{q}", [P, S], F32R) for q in "hl"] for p in range(2)]
            kt = [[sb(ph, f"kt{p}{q}", [P, S], F32R) for q in "hl"] for p in range(2)]
            prob = sb(ph, "prob", [P, 4, S])
            probt = [sb(ph, f"probt{p}", [P, 2, TB, S]) for p in range(2)]
            nmax = sb(ph, "nmax", [P, 2, NU])
            den = sb(ph, "den", [P, 2, NU])
            rden = sb(ph, "rden", [P, NU])
            rrep = sb(ph, "rrep", [P, TB, 2, HD])
            ones = sb(ph, "ones", [P, NU])
            ot = sb(ph, "ot", [P, S])
            s_hb = [sem("b_hb0"), sem("b_hb1")]
            (p_prj, p_tr, p_s, p_pt, p_o, p_r, p_out, a_raw, a_hi, a_exp, a_pt, a_r,
             v_max, v_pt, v_cos, v_lo, v_rden, v_ot, v_acc, g_sin, g_rot, g_rep, g_one) = (
                sem("b_" + n) for n in (
                    "prj", "tr", "s", "pt", "o", "r", "out", "araw", "ahi", "aexp", "apt",
                    "ar", "vmax", "vpt", "vcos", "vlo", "vrden", "vot", "vacc", "gsin", "grot", "grep", "gone"))
            bank_s, bank_pt, bank_o, bank_r = 2, 4, 6, 7
            BY_ACT = (1, 3, 5, 6, 7)

            def width(u):
                return (UNITS[u][1] + 1) * P

            def stored(n, u):
                mine = [x for x in range(NU) if (x in BY_ACT) == (u in BY_ACT)]
                return (a_pt if u in BY_ACT else v_pt), len(mine) * n + mine.index(u) + 1

            def work_bank(k):
                return ps[:, k % 2, :]

            def pe_project(e, n, par, t):
                nxt = 1 - par
                if t == 0:
                    wait(e, s_hb[nxt], 16 * (n + 1 - nxt) + 32)
                if t < 2:
                    wait(e, v_lo, 2 * n + 1 + t)
                else:
                    wait(e, a_raw, 4 * (n + 1) + t - 1)
                o = work_bank(t)[:, 0:384]
                cols = bass.ds(((n + 1) % HP) * 384, 384)
                hi, lo = (hb[nxt][q][:, t * P:(t + 1) * P] for q in range(2))
                e.matmul(o, hi, wq_hi[:, cols], start=True, stop=False)
                e.matmul(o, hi, wq_lo[:, cols], start=False, stop=False)
                e.matmul(o, lo, wq_hi[:, cols], start=False, stop=True).then_inc(p_prj, 1)

            def pe_turn(e, n, which):
                if which == 0:
                    wait(e, g_rot, 2 * (n + 2))
                wait(e, a_raw, 4 * (n + 1) + 3 + which)
                for t in range(TB):
                    mm = e.transpose(work_bank(which)[:, t * P:(t + 1) * P],
                                     qk[:, t, which * P:(which + 1) * P], ident[:])
                mm.then_inc(p_tr, 1)

            def pe_scores(e, n, par, u):
                g = NU * n + u
                if u == 0:
                    wait(e, v_lo, 2 * n + 2)
                wait(e, a_exp, g - 1)
                j, i = UNITS[u]
                w = width(u)
                o = ps[:, bank_s + u % 2, 0:w]
                rows = slice(j * HD, (j + 1) * HD)
                cols = slice(i * P, (i + 1) * P)
                e.matmul(o, qt[par][0][rows, cols], kt[par][0][rows, 0:w], start=True, stop=False)
                e.matmul(o, qt[par][1][rows, cols], kt[par][0][rows, 0:w], start=False, stop=False)
                e.matmul(o, qt[par][0][rows, cols], kt[par][1][rows, 0:w], start=False, stop=False)
                e.matmul(ps[:, bank_s + u % 2, w - P:w], ident_b[:], mask_b[:], start=False,
                         stop=True).then_inc(p_s, 1)

            def pe_turn_prob(e, n, u):
                wait(e, a_exp, NU * n + u + 1)
                wait(e, *(stored(n, u - 2) if u >= 2 else stored(n - 1, NU + u - 2)))
                for kk in range(UNITS[u][1] + 1):
                    mm = e.transpose(ps[:, bank_pt + u % 2, kk * P:(kk + 1) * P],
                                     prob[:, u % 4, kk * P:(kk + 1) * P], ident[:])
                mm.then_inc(p_pt, 1)

            def pe_values(e, n, par):
                wait(e, v_pt, (NU - len(BY_ACT)) * (n + 1))
                wait(e, a_pt, len(BY_ACT) * (n + 1))
                wait(e, v_ot, n)
                for kk in range(TB):
                    for j in range(2):
                        mm = e.matmul(ps[j * HD:(j + 1) * HD, bank_o, kk * P:S],
                                      raw[par][:, kk, 256 + j * HD:256 + (j + 1) * HD],
                                      probt[par][:, j, kk, kk * P:S], start=(kk == 0), stop=(kk == TB - 1))
                mm.then_inc(p_o, 1)

            def pe_turn_sum(e, n):
                wait(e, g_rep, n + 1)
                wait(e, v_acc, n)
                for i in range(TB):
                    mm = e.transpose(ps[:, bank_r, i * P:(i + 1) * P],
                                     rrep[:, i, :, :].rearrange("p j f -> p (j f)"), ident[:])
                mm.then_inc(p_r, 1)

            def pe_out(e, n):
                wait(e, v_ot, n + 1)
                for t in range(TB):
                    mm = e.matmul(ps[:, bank_r, t * P:(t + 1) * P], ot[:, t * P:(t + 1) * P],
                                  wo[:, bass.ds((n % HP) * E, E)], start=True, stop=True)
                mm.then_inc(p_out, 1)

            BEFORE, NOW, AFTER = range(3)

            def run(e, table, parts, n, par, when):
                for what, arg, of in table:
                    if when[of]:
                        parts[what](e, n, par, arg)

            PE_ORDER = [("project", 0, AFTER), ("turn_prob'", 7, BEFORE), ("scores", 0, NOW), ("values", 0, BEFORE),
                        ("project", 1, AFTER), ("scores", 1, NOW), ("project", 2, AFTER), ("scores", 2, NOW),
                        ("turn_prob", 0, NOW), ("project", 3, AFTER), ("scores", 3, NOW), ("scores", 4, NOW),
                        ("turn_prob", 1, NOW), ("scores", 5, NOW), ("turn_prob", 2, NOW), ("turn_prob", 3, NOW),
                        ("turn_sum", 0, BEFORE), ("scores", 6, NOW), ("turn_prob", 4, NOW), ("scores", 7, NOW),
                        ("turn", 0, AFTER), ("turn", 1, AFTER), ("out", 0, BEFORE), ("turn_prob", 5, NOW),
                        ("turn_prob", 6, NOW)]
            PE_PARTS = {
                "turn_prob'": lambda e, n, par, u: pe_turn_prob(e, n - 1, u),
                "turn_prob": lambda e, n, par, u: pe_turn_prob(e, n, u),
                "values": lambda e, n, par, _: pe_values(e, n - 1, 1 - par),
                "scores": pe_scores,
                "project": pe_project,
                "turn_sum": lambda e, n, par, _: pe_turn_sum(e, n - 1),
                "out": lambda e, n, par, _: pe_out(e, n - 1),
                "turn": lambda e, n, par, which: pe_turn(e, n, which)}

            def act_raw(e, n, par, t):
                m = n + 1
                wait(e, p_prj, 4 * m + t + 1)
                if t == 0:
                    wait(e, p_o, n)
                e.copy(raw[1 - par][:, t, :], work_bank(t)[:, 0:384]).then_inc(a_raw, 1)

            def act_hi(e, n, par, which):
                wait(e, p_tr, 2 * (n + 1) + which + 1)
                if which == 0:
                    wait(e, p_s, NU * n)
                dst = (qt, kt)[which][1 - par][0]
                e.copy(dst[:], work_bank(which)).then_inc(a_hi, 1)

            def act_exp(e, n, par, u):
                g = NU * n + u
                j, i = UNITS[u]
                wait(e, v_max, g + 1)
                wait(e, p_pt, g - 3)
                if u == 0:
                    wait(e, v_rden, n - 1)
                e.activation(prob[:, u % 4, 0:width(u)], ps[:, bank_s + u % 2, 0:width(u)], ACT.Exp,
                             bias=nmax[:, par, u:u + 1],
                             accum_out=den[:, par, 2 * i + j:2 * i + j + 1]).then_inc(a_exp, 1)

            def store_prob(e, n, par, u, copy):
                j, i = UNITS[u]
                wait(e, p_pt, NU * n + u + 1)
                if u < 2:
                    wait(e, p_o, n - 1)
                copy(probt[par][:, j, 0:i + 1, i * P:(i + 1) * P],
                     ps[:, bank_pt + u % 2, 0:width(u)].rearrange("p (k q) -> p k q", q=P))\
                    .then_inc(stored(0, u)[0], 1)

            def act_r(e, n):
                wait(e, p_r, n + 1)
                wait(e, p_out, n)
                e.copy(ot[:], ps[:, bank_r, :]).then_inc(a_r, 1)

            ACT_ORDER = [("store'", 5, BEFORE), ("store'", 6, BEFORE), ("store'", 7, BEFORE), ("exp", 0, NOW),
                         ("raw", 0, AFTER), ("raw", 1, AFTER), ("raw", 2, AFTER), ("exp", 1, NOW), ("exp", 2, NOW),
                         ("raw", 3, AFTER), ("exp", 3, NOW), ("store", 1, NOW), ("exp", 4, NOW), ("exp", 5, NOW),
                         ("sum", 0, BEFORE), ("store", 3, NOW), ("exp", 6, NOW), ("hi", 0, AFTER), ("hi", 1, AFTER),
                         ("exp", 7, NOW)]
            ACT_PARTS = {
                "store'": lambda e, n, par, u: store_prob(e, n - 1, 1 - par, u, e.copy),
                "store": lambda e, n, par, u: store_prob(e, n, par, u, e.copy),
                "exp": act_exp,
                "raw": act_raw,
                "sum": lambda e, n, par, _: act_r(e, n - 1),
                "hi": act_hi}

            def dve_max(e, n, par, u):
                wait(e, p_s, NU * n + u + 1)
                e.tensor_reduce(nmax[:, par, u:u + 1], ps[:, bank_s + u % 2, 0:width(u)], AX.X, ALU.max,
                                negate=True).then_inc(v_max, 1)

            def dve_cos(e, n, par, half):
                m = n + 1
                wait(e, a_raw, 4 * m + 2 * half + 2)
                wait(e, p_tr, 2 * m)
                t = slice(2 * half, 2 * half + 2)
                e.tensor_tensor(qk[:, t, :], raw[1 - par][:, t, 0:256], cos[:, t, :], op=ALU.mult).then_inc(v_cos, 1)

            def dve_lo(e, n, par, which):
                wait(e, a_hi, 2 * (n + 1) + which + 1)
                hi, lo = (qt, kt)[which][1 - par]
                e.tensor_tensor(lo[:], work_bank(which), hi[:], op=ALU.subtract).then_inc(v_lo, 1)

            def dve_rden(e, n, par):
                wait(e, a_exp, NU * (n + 1))
                wait(e, g_rep, n)
                e.reciprocal(rden[:], den[:, par, :]).then_inc(v_rden, 1)

            def dve_ot(e, n):
                wait(e, a_r, n + 1)
                wait(e, p_o, n + 1)
                e.tensor_tensor(ot[:], ps[:, bank_o, :], ot[:], op=ALU.mult).then_inc(v_ot, 1)

            def dve_acc(e, n):
                wait(e, p_out, n + 1)
                wait(e, v_acc, n)
                dst = acc[:, bass.ds((n // HP) * TB, TB), :]
                e.tensor_tensor(dst, ps[:, bank_r, :].rearrange("p (t f) -> p t f", t=TB), dst,
                                op=ALU.add).then_inc(v_acc, 1)

            DVE_ORDER = [("max", 0, NOW), ("rden", 0, BEFORE), ("max", 1, NOW), ("cos", 0, AFTER), ("max", 2, NOW),
                         ("store", 0, NOW), ("max", 3, NOW), ("cos", 1, AFTER), ("max", 4, NOW), ("max", 5, NOW),
                         ("store", 2, NOW), ("max", 6, NOW), ("ot", 0, BEFORE), ("max", 7, NOW), ("store", 4, NOW),
                         ("lo", 0, AFTER), ("lo", 1, AFTER), ("acc", 0, BEFORE)]
            DVE_PARTS = {
                "rden": lambda e, n, par, _: dve_rden(e, n - 1, 1 - par),
                "store'": lambda e, n, par, u: store_prob(e, n - 1, 1 - par, u, e.tensor_copy),
                "store": lambda e, n, par, u: store_prob(e, n, par, u, e.tensor_copy),
                "max": dve_max,
                "cos": dve_cos,
                "ot": lambda e, n, par, _: dve_ot(e, n - 1),
                "acc": lambda e, n, par, _: dve_acc(e, n - 1),
                "lo": dve_lo}

            def pool_rep(e, n):
                wait(e, v_rden, n + 1)
                wait(e, p_r, n)
                e.tensor_tensor(rrep[:].rearrange("p t j f -> p (t j) f"),
                                rden[:].unsqueeze(2).to_broadcast([P, NU, HD]),
                                ones[:].unsqueeze(2).to_broadcast([P, NU, HD]), op=ALU.mult).then_inc(g_rep, 1)

            def pool_rotate(e, n, par, half):
                m = n + 1
                t = slice(2 * half, 2 * half + 2)

                def part(x, k, width=256):
                    return x[:, t, 0:256].rearrange("p t (h k f) -> p t h k f", k=2, f=HD // 2)[:, :, :, k, :]
                wait(e, a_raw, 4 * m + 2 * half + 2)
                wait(e, g_rot, 2 * m - 1 + half)
                for k in range(2):
                    e.tensor_tensor(part(rot, k), part(raw[1 - par], 1 - k), part(sin, k), op=ALU.mult)\
                        .then_inc(g_sin, 1)
                wait(e, v_cos, 2 * m + half + 1)
                wait(e, g_sin, 4 * m + 2 * half + 2)
                e.tensor_tensor(qk[:, t, :], qk[:, t, :], rot[:, t, :], op=ALU.add).then_inc(g_rot, 1)

            POOL_ORDER = [("rep", 0, BEFORE), ("rotate", 0, AFTER), ("rotate", 1, AFTER)]
            POOL_PARTS = {"rep": lambda e, n, par, _: pool_rep(e, n - 1), "rotate": pool_rotate}

            def all_steps(e, table, parts):
                run(e, table, parts, -1, 1, (False, False, True))
                run(e, table, parts, 0, 0, (False, True, True))
                with e.Fori(0, (STEPS - 2) // 2) as i:
                    run(e, table, parts, 2 * i + 1, 1, (True, True, True))
                    run(e, table, parts, 2 * i + 2, 0, (True, True, True))
                run(e, table, parts, STEPS - 1, 1, (True, True, False))
                run(e, table, parts, STEPS, 0, (True, False, False))

            with nc.Block() as block:
                @block.sync
                def _(e):
                    def load(m, par):
                        cols = bass.ds(e.snap((m // HP) * S) if not isinstance(m, int) else (m // HP) * S, S)
                        wait(e, p_prj, 4 * (m - 1))
                        for q, src in enumerate((h_hi, h_lo)):
                            e.dma_start(hb[par][q][:].bitcast(F32), src[:, cols].bitcast(F32))\
                                .then_inc(s_hb[par], 16)
                    in_pairs(e, STEPS, load)

                @block.tensor
                def _(e):
                    all_steps(e, PE_ORDER, PE_PARTS)

                @block.scalar
                def _(e):
                    all_steps(e, ACT_ORDER, ACT_PARTS)

                @block.vector
                def _(e):
                    all_steps(e, DVE_ORDER, DVE_PARTS)

                @block.gpsimd
                def _(e):
                    e.memset(ones[:], 1.0).then_inc(g_one, 1)
                    wait(e, g_one, 1)
                    all_steps(e, POOL_ORDER, POOL_PARTS)
        att.close()

        ffn = ctx.enter_context(ExitStack())
        h2 = sb(ffn, "h2", [P, NT, E])
        logits = sb(ffn, "logits", [P, NT, NX])
        share = sb(ffn, "share", [P, NT, NX])
        wu = [sb(ffn, f"wu{q}", [P, NX * I], F32R) for q in "hl"]
        wd = [sb(ffn, f"wd{q}", [P, NX * IC * E], F32R) for q in "hl"]
        with ExitStack() as ph:
            WH = NX * I // 2
            wtmp = sb(ph, "wtmp", [P, 2, WH])
            xh = sb(ph, "xh3", [P, 2, TB, E])
            hn = sb(ph, "hn3", [P, 2, TB, E])
            ht = sb(ph, "ht3", [P, 2, S])
            t1 = sb(ph, "t1", [P, 2, TB, E])
            r8 = sb(ph, "r8", [P, 4, NT, NX])
            r1 = sb(ph, "r1", [P, 4, NT])
            (d_w, s_t1, s_x1, s_st, s_dve, s_var, s_root, s_xh, s_mul, s_hn, s_keep, s_tr, s_ht, s_hi, s_lo,
             s_lg, s_lgs, s_whi, s_wlo, s_e) = (
                sem("c_" + n) for n in ("dw", "t1", "x1", "st", "dve", "var", "root", "xh", "mul", "hn", "keep",
                                        "tr", "ht", "hi", "lo", "lg", "lgs", "whi", "wlo", "e"))
            with nc.Block() as block:
                @block.sync
                def _(e):
                    for q in range(4):
                        wait(e, d_w, 16 * q)
                        wait(e, s_wlo, q - 1)
                        e.dma_start(wtmp[:, q % 2, :], (w_up, w_down)[q // 2][:, q % 2 * WH:(q % 2 + 1) * WH])\
                            .then_inc(d_w, 16)

                @block.gpsimd
                def _(e):
                    for q in range(4):
                        wait(e, s_whi, q + 1)
                        cols = slice(q % 2 * WH, (q % 2 + 1) * WH)
                        e.tensor_tensor((wu, wd)[q // 2][1][:, cols], wtmp[:, q % 2, :],
                                        (wu, wd)[q // 2][0][:, cols], op=ALU.subtract).then_inc(s_wlo, 1)

                    def batch(b, par):
                        rows = bass.ds(b * TB, TB)
                        wait(e, s_x1, b - 1)
                        e.tensor_tensor(t1[:, par], acc[:, rows, :],
                                        mod[:, bass.ds(b, 1), 0:1, :].rearrange("p a c f -> p (a c) f")
                                        .to_broadcast([P, TB, E]), op=ALU.mult).then_inc(s_t1, 1)
                    in_pairs(e, B, batch)
                    def batch(b, par):
                        wait(e, s_xh, b + 1)
                        e.tensor_tensor(xh[:, par], xh[:, par],
                                        mod[:, bass.ds(b, 1), 2:3, :].rearrange("p a c f -> p (a c) f")
                                        .to_broadcast([P, TB, E]), op=ALU.mult).then_inc(s_mul, 1)
                        wait(e, s_mul, b + 1)
                        wait(e, s_tr, b - 1)
                        wait(e, s_keep, b - 1)
                        e.tensor_tensor(hn[:, par], xh[:, par],
                                        mod[:, bass.ds(b, 1), 1:2, :].rearrange("p a c f -> p (a c) f")
                                        .to_broadcast([P, TB, E]), op=ALU.add).then_inc(s_hn, 1)
                    in_pairs(e, B, batch)

                @block.scalar
                def _(e):
                    for q in range(4):
                        wait(e, d_w, 16 * (q + 1))
                        e.copy((wu, wd)[q // 2][0][:, q % 2 * WH:(q % 2 + 1) * WH], wtmp[:, q % 2, :]).then_inc(s_whi, 1)
                    wait(e, s_var, 1)
                    e.activation(tmp[:, 3, :], tmp[:, 1, :], ACT.Sqrt).then_inc(s_root, 1)
                    def batch(b, par):
                        wait(e, s_hn, b + 1)
                        e.copy(h2[:, bass.ds(b * TB, TB), :], hn[:, par]).then_inc(s_keep, 1)
                        wait(e, s_tr, b + 1)
                        wait(e, s_lo, b - 1)
                        wait(e, s_lg, b - 1)
                        e.copy(ht[:, par, :], ps[:, par, :]).then_inc(s_ht, 1)
                    in_pairs(e, B, batch)
                    wait(e, s_dve, 12)
                    e.activation(r8[:, 1].rearrange("p n x -> p (n x)"), r8[:, 0].rearrange("p n x -> p (n x)"),
                                 ACT.Exp).then_inc(s_e, 1)

                @block.tensor
                def _(e):
                    def batch(b, par):
                        wait(e, s_hn, b + 1)
                        wait(e, s_ht, b - 1)
                        for t in range(TB):
                            mm = e.transpose(ps[:, par, t * P:(t + 1) * P], hn[:, par, t, :], ident[:])
                        mm.then_inc(s_tr, 1)
                        wait(e, s_ht, b + 1)
                        wait(e, s_lgs, b - 1)
                        for t in range(TB):
                            mm = e.matmul(ps[:, 2 + par, t * NX:(t + 1) * NX], ht[:, par, t * P:(t + 1) * P],
                                          gate_sb[:], start=True, stop=True)
                        mm.then_inc(s_lg, 1)
                    in_pairs(e, B, batch)

                @block.vector
                def _(e):
                    k = [0]

                    def step(ins):
                        ins.then_inc(s_dve, 1)
                        k[0] += 1
                        wait(e, s_dve, k[0])
                    def batch(b, par):
                        rows = bass.ds(b * TB, TB)
                        wait(e, s_t1, b + 1)
                        e.tensor_tensor(x_all[:, rows, :], x_all[:, rows, :], t1[:, par],
                                        op=ALU.add).then_inc(s_x1, 1)
                    in_pairs(e, B, batch)
                    wait(e, s_x1, B)

                    def batch(b, par):
                        for t in range(TB):
                            e.bn_stats(stats[:, bass.ds(b * TB + t, 1), :].rearrange("p a f -> p (a f)"),
                                       x_all[:, bass.ds(b * TB + t, 1), :].rearrange("p a f -> p (a f)"))\
                                .then_inc(s_st, 1)
                    in_pairs(e, B, batch)
                    wait(e, s_st, NT)
                    t3 = (tmp[:, 0, :], tmp[:, 1, :], tmp[:, 2, :])
                    finish_stats(e, s_dve, stats, mean[:], rstd[:], None, t3, 0, s_var, s_root)
                    k[0] = 6
                    wait(e, s_root, 1)
                    finish_root(e, step, tmp[:, 3, :], rstd[:], t3)
                    def batch(b, par):
                        wait(e, s_hn, b - 1)
                        for t in range(TB):
                            ts = e.tensor_scalar(xh[:, par, t, :],
                                                 x_all[:, bass.ds(b * TB + t, 1), :].rearrange("p a f -> p (a f)"),
                                                 mean[:, bass.ds(b * TB + t, 1)], rstd[:, bass.ds(b * TB + t, 1)],
                                                 ALU.subtract, ALU.mult)
                        ts.then_inc(s_xh, 1)
                        wait(e, s_ht, b + 1)
                        cols = bass.ds(b * S, S)
                        e.tensor_copy(h_hi[:, cols], ht[:, par, :]).then_inc(s_hi, 1)
                        wait(e, s_hi, b + 1)
                        e.tensor_tensor(h_lo[:, cols], ht[:, par, :], h_hi[:, cols],
                                        op=ALU.subtract).then_inc(s_lo, 1)
                        wait(e, s_lg, b + 1)
                        e.tensor_tensor(logits[:, bass.ds(b * TB, TB), :],
                                        ps[:, 2 + par, 0:TB * NX].rearrange("p (t x) -> p t x", x=NX),
                                        bias_sb[:].unsqueeze(1).to_broadcast([P, TB, NX]),
                                        op=ALU.add).then_inc(s_lgs, 1)
                    in_pairs(e, B, batch)
                    wait(e, s_lgs, B)

                    def over(a):
                        return a.unsqueeze(2).to_broadcast([P, NT, NX])
                    rk = rank[:].unsqueeze(1).to_broadcast([P, NT, NX])
                    top = r1[:, 0, :]
                    e.tensor_reduce(top, logits[:], AX.X, ALU.max).then_inc(s_lgs, 1)
                    wait(e, s_lgs, B + 1)
                    step(e.tensor_tensor(r8[:, 0], logits[:], over(top), op=ALU.subtract))
                    assert k[0] == 12
                    wait(e, s_e, 1)
                    step(e.tensor_reduce(r1[:, 1, :], r8[:, 1], AX.X, ALU.add))
                    step(e.reciprocal(r1[:, 2, :], r1[:, 1, :]))
                    step(e.tensor_tensor(r8[:, 1], r8[:, 1], over(r1[:, 2, :]), op=ALU.mult))
                    chosen = share[:]
                    for turn in range(2):
                        best = r1[:, turn, :]
                        step(e.tensor_reduce(best, r8[:, 1], AX.X, ALU.max))
                        step(e.tensor_tensor(r8[:, 2], r8[:, 1], over(best), op=ALU.is_equal))
                        step(e.tensor_tensor(r8[:, 2], r8[:, 2], rk, op=ALU.mult))
                        step(e.tensor_reduce(r1[:, 2, :], r8[:, 2], AX.X, ALU.max))
                        step(e.tensor_tensor(r8[:, 2], rk, over(r1[:, 2, :]), op=ALU.is_equal))
                        step(e.scalar_tensor_tensor(out=r8[:, 1], in0=r8[:, 2], scalar=-2.0, in1=r8[:, 1],
                                                    op0=ALU.mult, op1=ALU.add))
                        if turn == 0:
                            step(e.tensor_tensor(chosen, r8[:, 2], over(best), op=ALU.mult))
                        else:
                            step(e.tensor_tensor(r8[:, 3], r8[:, 2], over(best), op=ALU.mult))
                            step(e.tensor_tensor(chosen, chosen, r8[:, 3], op=ALU.add))
                    step(e.tensor_tensor(r1[:, 2, :], r1[:, 0, :], r1[:, 1, :], op=ALU.add))
                    step(e.tensor_scalar(r1[:, 2, :], r1[:, 2, :], GATE_EPS, None, ALU.add))
                    step(e.reciprocal(r1[:, 3, :], r1[:, 2, :]))
                    step(e.tensor_tensor(chosen, chosen, over(r1[:, 3, :]), op=ALU.mult))

        with ExitStack() as ph:
            NC = NX * IC
            hf = sb(ph, "hf", [P, 4, S])
            hh = sb(ph, "hh", [P, 4, S], F32R)
            hl = sb(ph, "hl", [P, 4, S], F32R)
            st4 = sb(ph, "st4", [P, TB, 6])
            m4 = sb(ph, "m4", [P, TB])
            r4 = sb(ph, "r4", [P, TB])
            t4 = sb(ph, "t4", [P, 4, TB])
            y4 = sb(ph, "y4", [P, TB, E])
            pause = sb(ph, "pause", [P, 1])
            yt = sb(ph, "yt", [P, 2, S])
            (p_up, p_dn, p_ty, a_y, a_ge, a_hi, v_hi, v_lo, v_acc, v_st, v_var, a_root, v_y, g_y, d_out) = (
                sem("d_" + n) for n in ("up", "dn", "ty", "ay", "ge", "ahi", "hi", "lo", "acc", "st", "var", "root", "y", "gy", "out"))
            LAG = 3
            bank_y, bank_t = 4, 6

            def up(e, n, k):
                g = NC * n + k
                wait(e, a_ge, g - 3)
                o = ps[:, k % 4, :]
                w = slice(k * P, (k + 1) * P)
                cols = bass.ds(n * S, S)
                e.matmul(o, wu[0][:, w], h_hi[:, cols], start=True, stop=False)
                e.matmul(o, wu[0][:, w], h_lo[:, cols], start=False, stop=False)
                e.matmul(o, wu[1][:, w], h_hi[:, cols], start=False, stop=True).then_inc(p_up, 1)

            def down(e, n, k):
                g = NC * n + k
                x, c = divmod(k, IC)
                wait(e, v_lo, g + 1)
                if c == 0:
                    wait(e, a_y, NX * n + x - 1)
                w = slice(k * E, (k + 1) * E)
                o = ps[:, bank_y + x % 2, :]
                e.matmul(o, wd[0][:, w], hh[:, k % 4, :], start=(c == 0), stop=False)
                e.matmul(o, wd[0][:, w], hl[:, k % 4, :], start=False, stop=False)
                e.matmul(o, wd[1][:, w], hh[:, k % 4, :], start=False, stop=(c == IC - 1)).then_inc(p_dn, 1)

            def turn_y(e, n, x):
                wait(e, a_y, NX * n + x + 1)
                wait(e, v_acc, NX * n + x - 1)
                for t in range(TB):
                    mm = e.transpose(ps[:, bank_t + x % 2, t * P:(t + 1) * P], yt[:, x % 2, t * P:(t + 1) * P],
                                     ident[:])
                mm.then_inc(p_ty, 1)

            def each(k, lag, now, before, n, act):
                q = k - lag
                if q % IC == IC - 1:
                    if q >= 0 and now:
                        act(n, q // IC)
                    if q < 0 and before:
                        act(n - 1, NX + q // IC)

            def pe4(e, n, now=True, before=True):
                for k in range(NC):
                    if now:
                        up(e, n, k)
                    if k >= LAG:
                        if now:
                            down(e, n, k - LAG)
                    elif before:
                        down(e, n - 1, NC - LAG + k)
                    each(k, LAG + 2, now, before, n, lambda m, x: turn_y(e, m, x))

            def store_y(e, n, x):
                wait(e, p_dn, NC * n + IC * (x + 1))
                wait(e, p_ty, NX * n + x - 1)
                e.copy(yt[:, x % 2, :], ps[:, bank_y + x % 2, :]).then_inc(a_y, 1)

            def act4(e, n, now=True, before=True):
                for k in range(NC):
                    if now:
                        g = NC * n + k
                        wait(e, p_up, g + 1)
                        wait(e, v_lo, g - 3)
                        e.activation(hf[:, k % 4, :], ps[:, k % 4, :], ACT.Gelu).then_inc(a_ge, 1)
                        if k % 2:
                            wait(e, a_ge, g + 1)
                            wait(e, p_dn, g - 3)
                            e.copy(hh[:, k % 4, :], hf[:, k % 4, :]).then_inc(a_hi, 1)
                    each(k, LAG + 1, now, before, n, lambda m, x: store_y(e, m, x))
                    if before and k == 11:
                        wait(e, v_var, n)
                        e.activation(t4[:, 3, :], t4[:, 1, :], ACT.Sqrt).then_inc(a_root, 1)

            def add_up(e, n, x):
                wait(e, p_ty, NX * n + x + 1)
                wait(e, v_acc, NX * n + x)
                for t in range(TB):
                    dst = acc[:, bass.ds(n * TB + t, 1), :].rearrange("p a f -> p (a f)")
                    src = ps[:, bank_t + x % 2, t * P:(t + 1) * P]
                    wt = share[:, bass.ds(n * TB + t, 1), x:x + 1].rearrange("p a f -> p (a f)")
                    if x == 0:
                        ins = e.tensor_scalar(dst, src, wt, None, ALU.mult)
                    else:
                        ins = e.scalar_tensor_tensor(out=dst, in0=src, scalar=wt, in1=dst, op0=ALU.mult, op1=ALU.add)
                ins.then_inc(v_acc, 1)

            NV = 6 + 5

            def dve4(e, n, now=True, before=True):
                for k in range(NC):
                    if now:
                        g = NC * n + k
                        wait(e, p_dn, g - 3)
                        if k % 2:
                            wait(e, a_hi, (NC // 2) * n + k // 2 + 1)
                        else:
                            wait(e, a_ge, g + 1)
                            e.tensor_copy(hh[:, k % 4, :], hf[:, k % 4, :]).then_inc(v_hi, 1)
                            wait(e, v_hi, (NC // 2) * n + k // 2 + 1)
                        e.tensor_tensor(hl[:, k % 4, :], hf[:, k % 4, :], hh[:, k % 4, :],
                                        op=ALU.subtract).then_inc(v_lo, 1)
                    each(k, LAG + 2, now, before, n, lambda m, x: add_up(e, m, x))
                    if before and k == 6:
                        m = n - 1
                        wait(e, v_acc, NX * n)
                        e.memset(pause[:], 0.0)
                        for t in range(TB):
                            e.bn_stats(st4[:, t, :], acc[:, bass.ds(m * TB + t, 1), :].rearrange("p a f -> p (a f)"))\
                                .then_inc(v_st, 1)
                        base = (TB + NV) * m + TB
                        wait(e, v_st, base)
                        t3 = (t4[:, 0, :], t4[:, 1, :], t4[:, 2, :])
                        finish_stats(e, v_st, st4, m4[:], r4[:], None, t3, base, v_var, a_root)
                    if before and k == 13:
                        m = n - 1
                        at = [(TB + NV) * m + TB + 6]

                        def step(ins):
                            ins.then_inc(v_st, 1)
                            at[0] = at[0] + 1
                            wait(e, v_st, at[0])
                        wait(e, a_root, n)
                        finish_root(e, step, t4[:, 3, :], r4[:], (t4[:, 0, :], t4[:, 1, :], t4[:, 2, :]))
                        wait(e, g_y, 3 * m)
                        for t in range(TB):
                            ts = e.tensor_scalar(y4[:, t, :], acc[:, bass.ds(m * TB + t, 1), :].rearrange("p a f -> p (a f)"),
                                                 m4[:, t:t + 1], r4[:, t:t + 1], ALU.subtract, ALU.mult)
                        ts.then_inc(v_y, 1)

            def pool4(e, m):
                rows = bass.ds(m * TB, TB)
                wait(e, v_y, m + 1)
                e.tensor_tensor(y4[:], y4[:], h2[:, rows, :], op=ALU.add).then_inc(g_y, 1)
                wait(e, g_y, 3 * m + 1)
                e.tensor_tensor(y4[:], y4[:], mod[:, bass.ds(m, 1), 3:4, :].rearrange("p a c f -> p (a c) f")
                                .to_broadcast([P, TB, E]), op=ALU.mult).then_inc(g_y, 1)
                wait(e, g_y, 3 * m + 2)
                e.tensor_tensor(x_all[:, rows, :], x_all[:, rows, :], y4[:], op=ALU.add).then_inc(g_y, 1)

            def all_batches(e, step):
                step(e, 0, before=False)
                with e.Fori(1, B) as n:
                    step(e, n)
                step(e, B, now=False)

            with nc.Block() as block:
                @block.tensor
                def _(e):
                    all_batches(e, pe4)

                @block.scalar
                def _(e):
                    all_batches(e, act4)

                @block.vector
                def _(e):
                    all_batches(e, dve4)

                @block.gpsimd
                def _(e):
                    with e.Fori(0, B) as m:
                        pool4(e, m)

                @block.sync
                def _(e):
                    ov = out.rearrange("(n p) f -> p n f", p=P)
                    with e.Fori(0, B) as m:
                        wait(e, g_y, 3 * m + 3)
                        e.dma_start(ov[:, bass.ds(m * TB, TB), :], x_all[:, bass.ds(m * TB, TB), :]).then_inc(d_out, 16)
                    wait(e, d_out, 16 * B)


def kernel(L0_attn_x, L0_attn_W_qkv, L0_attn_W_out, L0_ffn_gate_w, L0_ffn_expert_bias, L0_ffn_w_up, L0_ffn_w_down,
           L0_c, L0_wmod):
    import numpy as np
    import concourse.bacc as bacc
    from concourse.bass_utils import run_bass_kernel_spmd

    w = np.asarray(L0_attn_W_qkv).reshape(E, 3, HP, 2, HD)
    order = np.concatenate([np.arange(0, HD, 2), np.arange(1, HD, 2)])
    w = np.stack([w[:, 0][..., order], w[:, 1][..., order], w[:, 2]], axis=2)
    freqs = (1.0 / np.float32(10000.0) ** (np.arange(0, HD, 2) / HD).astype(np.float32)).astype(np.float32)
    angles = np.arange(S, dtype=np.float32)[:, None] * freqs[None, :]
    co, si = np.cos(angles), np.sin(angles)
    scale = np.repeat(np.array([HD ** -0.5, 1.0], np.float32), 2)[None, :, None]
    cos4 = np.concatenate([co, co], 1)[:, None, :] * scale
    sin4 = np.concatenate([-si, si], 1)[:, None, :] * scale

    def by_tile(a):
        return np.ascontiguousarray(a.reshape(TB, P, 256).transpose(1, 0, 2).reshape(P, TB * 256), np.float32)
    arrays = {
        "x": np.asarray(L0_attn_x).reshape(B * S, E),
        "w_qkv": np.ascontiguousarray(w.reshape(E, HP * 384)),
        "w_out": np.asarray(L0_attn_W_out),
        "gate_w": np.ascontiguousarray(np.asarray(L0_ffn_gate_w).T),
        "expert_bias": np.asarray(L0_ffn_expert_bias),
        "w_up": np.ascontiguousarray(np.asarray(L0_ffn_w_up).transpose(2, 0, 1).reshape(E, NX * I)),
        "w_down": np.ascontiguousarray(np.asarray(L0_ffn_w_down).reshape(NX, E, IC, P).transpose(3, 0, 2, 1)
                                       .reshape(P, NX * IC * E)),
        "c_t": np.ascontiguousarray(np.asarray(L0_c).T),
        "w_mod": np.asarray(L0_wmod),
        "cos": by_tile(cos4),
        "sin": by_tile(sin4),
        "ident": np.eye(P, dtype=np.float32),
        "mask": np.triu(np.full((P, P), MASKED, np.float32), 1),
        "rank": np.tile(np.arange(NX, 0, -1, dtype=np.float32), (P, 1)),
    }
    nc = bacc.Bacc("TRN2", target_bir_lowering=False, num_devices=1)
    args = [nc.dram_tensor("in_" + name, a.shape, mybir.dt.from_np(a.dtype), kind="ExternalInput").ap()
            for name, a in arrays.items()]
    args.append(nc.dram_tensor("out", (B * S, E), F32, kind="ExternalOutput").ap())
    adaln_kernel(nc, *args)
    r = run_bass_kernel_spmd(nc, [{"in_" + name: a for name, a in arrays.items()}], core_ids=[0])
    return r.results[0]["out"].reshape(B, S, E)
```

```python
from contextlib import ExitStack

import concourse.bass as bass
from concourse import mybir

F32 = mybir.dt.float32
F32R = mybir.dt.float32r
BF16 = mybir.dt.bfloat16
ACT = mybir.ActivationFunctionType
ALU = mybir.AluOpType
AX = mybir.AxisListType

P = 128
B, S, E = 8, 512, 128
NT = B * S // P
TB = S // P
NH, HD = 16, 64
HP = NH // 2
STEPS = B * HP
NX, I = 8, 512
IC = I // P
RING = 4
NQ = NT // 4
GROUPS = ((0, NQ), (NQ, NT))
WH = NX * I // 2
GATE_EPS, LN_EPS = 1e-6, 1e-5
MASKED = -1e30
UNITS = [(j, i) for i in (3, 0, 2, 1) for j in (0, 1)]
NU = len(UNITS)


def wait(engine, semaphore, value):
    if not isinstance(value, int) or value > 0:
        engine.wait_ge(semaphore, value)


def adaln_kernel(nc, x_in, w_qkv, w_out, gate_w, expert_bias, w_up, w_down, c_t, w_mod,
                 cos_in, sin_in, ident_in, mask_in, rank_in, out):
    ctx = ExitStack()
    with ctx:
        def sem(name):
            return ctx.enter_context(nc.semaphore(name))

        def sb(scope, name, shape, dt=F32):
            return scope.enter_context(nc.sbuf_tensor(name, shape, dt))

        ps = ctx.enter_context(nc.psum_tensor("ps", [P, 8, 512], F32))
        x_all = sb(ctx, "x_all", [P, NT, E])
        h_hi = sb(ctx, "h_hi", [P, NT * P], F32R)
        h_lo = sb(ctx, "h_lo", [P, NT * P], F32R)
        rows4 = sb(ctx, "rows4", [B, 4, E])
        ident = sb(ctx, "ident", [P, P])
        stats = sb(ctx, "stats", [P, NT, 6])
        mean = sb(ctx, "mean", [P, NT])
        rstd = sb(ctx, "rstd", [P, NT])
        tmp = sb(ctx, "tmp", [P, 4, NT])
        numbers = sb(ctx, "numbers", [P, 5, TB])
        pause = sb(ctx, "pause", [P, 2])
        w_raw = sb(ctx, "w_raw", [P, WH])
        (d_x0, d_x1, d_x2, d_x3, d_late, d_e0, d_e1, d_e2, d_e3) = (
            sem(n) for n in ("d_x0", "d_x1", "d_x2", "d_x3", "d_late", "d_e0", "d_e1", "d_e2", "d_e3"))
        d_x, d_e = (d_x0, d_x1, d_x2, d_x3), (d_e0, d_e1, d_e2, d_e3)

        def chain(engine, done, base=0):
            count = [base]

            def step(*instructions):
                for ins in instructions:
                    ins.then_inc(done, 1)
                    count[0] = count[0] + 1
                wait(engine, done, count[0])
            return step

        NORM_STEPS = 14
        HALF, OVER_E, EPS, MINUS_HALF, ONE_AND_HALF = range(5)
        NUMBERS = (0.5, 1.0 / E, LN_EPS, -0.5, 1.5)

        def norm_factors(step, e, st, mean_, rstd_, t):
            t0, t1, t2 = t

            def k(i):
                return numbers[:, i, 0:t0.shape[-1]]
            step(e.tensor_tensor(t0, st(1), st(4), op=ALU.subtract),
                 e.tensor_tensor(t1, st(1), st(4), op=ALU.add),
                 e.tensor_tensor(t2, st(2), st(5), op=ALU.add))
            step(e.tensor_tensor(t0, t0, k(HALF), op=ALU.mult),
                 e.tensor_tensor(mean_, t1, k(HALF), op=ALU.mult),
                 e.tensor_tensor(t2, t2, k(OVER_E), op=ALU.mult))
            step(e.tensor_tensor(t0, t0, t0, op=ALU.mult),
                 e.tensor_tensor(t2, t2, k(EPS), op=ALU.add))
            step(e.tensor_tensor(t1, t0, t2, op=ALU.add))
            step(e.tensor_tensor(t2, t1, k(MINUS_HALF), op=ALU.pow))
            step(e.tensor_tensor(t0, t2, t2, op=ALU.mult))
            step(e.tensor_tensor(t0, t0, t1, op=ALU.mult))
            step(e.tensor_tensor(t0, t0, k(MINUS_HALF), op=ALU.mult))
            step(e.tensor_tensor(t0, t0, k(ONE_AND_HALF), op=ALU.add))
            return e.tensor_tensor(rstd_, t2, t0, op=ALU.mult)

        def factors_begin(step, e, st, mean_, t):
            t0, t1, t2 = t
            step(e.tensor_tensor(t0, st(1), st(4), op=ALU.subtract),
                 e.tensor_tensor(t1, st(1), st(4), op=ALU.add),
                 e.tensor_tensor(t2, st(2), st(5), op=ALU.add))
            step(e.tensor_scalar(mean_, t1, 0.5, None, ALU.mult),
                 e.tensor_tensor(t0, t0, t0, op=ALU.mult),
                 e.tensor_scalar(t2, t2, 1.0 / E, LN_EPS, ALU.mult, ALU.add))
            return e.scalar_tensor_tensor(out=t1, in0=t0, scalar=0.25, in1=t2, op0=ALU.mult, op1=ALU.add)

        def factors_end(step, e, rstd_, root, t):
            t0, t1, t2 = t
            step(e.reciprocal(t2, root))
            step(e.tensor_tensor(t0, t2, t2, op=ALU.mult))
            step(e.tensor_tensor(t0, t0, t1, op=ALU.mult))
            step(e.tensor_scalar(t0, t0, -0.5, 1.5, ALU.mult, ALU.add))
            return e.tensor_tensor(rstd_, t2, t0, op=ALU.mult)

        def group(g):
            first, last = GROUPS[g]
            rows = slice(first, last)
            return (lambda k: stats[:, rows, k]), mean[:, rows], rstd[:, rows], \
                [tmp[:, i, rows] for i in range(3)], tmp[:, 3, rows], last

        def group_begin(e, step, g, s_st, s_var):
            st, mean_, rstd_, t, root, last = group(g)
            wait(e, s_st, last)
            factors_begin(step, e, st, mean_, t).then_inc(s_var, 1)

        def group_end(e, step, g, s_root):
            st, mean_, rstd_, t, root, last = group(g)
            wait(e, s_root, g + 1)
            step(factors_end(step, e, rstd_, root, t))

        def group_root(e, g, s_var, s_root):
            st, mean_, rstd_, t, root, last = group(g)
            wait(e, s_var, g + 1)
            e.activation(root, t[1], ACT.Sqrt).then_inc(s_root, 1)

        def low_parts(e, ht, s_hi, s_lo):
            for b in range(B):
                wait(e, s_hi, b + 1)
                cols = slice(b * S, (b + 1) * S)
                e.tensor_tensor(h_lo[:, cols], ht[:, b % RING, :], h_hi[:, cols], op=ALU.subtract).then_inc(s_lo, 1)

        def normalise(e, b, out_):
            for t in range(TB):
                ins = e.tensor_scalar(out_[:, t, :], x_all[:, bass.ds(b * TB + t, 1), :].rearrange("p a f -> p (a f)"),
                                      mean[:, bass.ds(b * TB + t, 1)], rstd[:, bass.ds(b * TB + t, 1)],
                                      ALU.subtract, ALU.mult)
            return ins

        att = ctx.enter_context(ExitStack())
        wq_hi = sb(att, "wq_hi", [P, HP * 384], F32R)
        wq_lo = sb(att, "wq_lo", [P, HP * 384], F32R)
        wo = sb(att, "wo", [P, HP * E])
        ga = sb(att, "ga", [P, B, E])
        cos = sb(att, "cos", [P, TB, 256])
        sin = sb(att, "sin", [P, TB, 256])
        ident_b = sb(att, "ident_b", [P, P], BF16)
        mask_b = sb(att, "mask_b", [P, P], BF16)

        hb = [[sb(att, f"hb{p}{q}", [P, S], F32R) for q in "hl"] for p in range(2)]
        s_hb = [sem("b_hb0"), sem("b_hb1")]

        def load_h(e, cols, par):
            for q, src in enumerate((h_hi, h_lo)):
                e.dma_start(hb[par][q][:].bitcast(F32), src[:, cols].bitcast(F32)).then_inc(s_hb[par], 16)

        with ExitStack() as ph:
            wq_f = sb(ph, "wq_f", [P, HP * 384])
            mask_f = sb(ph, "mask_f", [P, P])
            ct = sb(ph, "ct", [P, 3, B])
            wm = sb(ph, "wm", [P, 6 * E])
            mod1 = sb(ph, "mod1", [P, 2, B])
            gt = sb(ph, "gt", [B, 2, E])
            xh = sb(ph, "xh1", [P, 2, TB, E])
            ht = sb(ph, "ht1", [P, RING, S])
            (d_c, d_m, d_w, d_i, d_k, s_exp, s_silu, s_mm, s_mod, s_rows, s_ga, s_st, s_dve, s_var, s_root, s_xh,
             s_tr, s_hi, s_ht, s_lo, s_whi, s_wlo, s_gb, s_num) = (
                sem("a_" + n) for n in (
                    "dc", "dm", "dw", "di", "dk", "exp", "silu", "mm", "mod", "rows", "ga", "st", "dve", "var", "root",
                    "xh", "tr", "hi", "ht", "lo", "whi", "wlo", "gb",
                    "num"))
            with nc.Block() as block:
                @block.sync
                def _(e):
                    e.dma_start(ct[:, 0, :], c_t).then_inc(d_c, 16)
                    xv = x_in.rearrange("(n p) f -> p n f", p=P)
                    for q in range(4):
                        e.dma_start(x_all[:, NQ * q:NQ * (q + 1), :], xv[:, NQ * q:NQ * (q + 1), :])\
                            .then_inc(d_x[q], 16)
                    e.dma_start(cos[:].rearrange("p t f -> p (t f)"), cos_in).then_inc(d_late, 16)
                    e.dma_start(sin[:].rearrange("p t f -> p (t f)"), sin_in).then_inc(d_late, 16)
                    e.dma_start(wo[:].rearrange("p (h f) -> p h f", h=HP),
                                w_out.rearrange("(h p) f -> p h f", p=P)).then_inc(d_late, 16)
                    wait(e, s_hi, 1)
                    wait(e, s_lo, 1)
                    for step in range(2):
                        load_h(e, slice(0, S), step)

                @block.scalar
                def _(e):
                    e.dma_start(wm[:], w_mod).then_inc(d_m, 16)
                    e.dma_start(ident[:], ident_in).then_inc(d_i, 16)
                    e.dma_start(wq_f[:], w_qkv).then_inc(d_w, 16)
                    e.dma_start(mask_f[:], mask_in).then_inc(d_k, 16)
                    wait(e, d_c, 16)
                    e.activation(ct[:, 1, :], ct[:, 0, :], ACT.Exp, scale=-1.0).then_inc(s_exp, 1)
                    group_root(e, 0, s_var, s_root)
                    wait(e, d_w, 16)
                    e.copy(wq_hi[:], wq_f[:]).then_inc(s_whi, 1)
                    group_root(e, 1, s_var, s_root)
                    wait(e, s_gb, 1)
                    e.copy(ga[:].rearrange("p b f -> p (b f)"),
                           ps[:, 4:6, :].rearrange("p b f -> p (b f)")).then_inc(s_ga, 1)
                    wait(e, s_mod, 2)
                    for b in range(B):
                        wait(e, s_tr, b + 1)
                        wait(e, s_lo, b - RING + 1)
                        e.activation(ht[:, b % RING, :], ps[:, b % 2, :], ACT.Identity, bias=mod1[:, 0, b:b + 1],
                                     scale=mod1[:, 1, b:b + 1]).then_inc(s_ht, 1)

                @block.tensor
                def _(e):
                    wait(e, s_silu, 1)
                    wait(e, d_m, 16)
                    for i in range(2):
                        e.matmul(ps[:, 3, i * B:(i + 1) * B], wm[:, i * E:(i + 1) * E], ct[:, 1, :], start=True,
                                 stop=True).then_inc(s_mm, 1)
                    e.matmul(ps[0:B, 2, :], ct[:, 1, :], wm[:, 2 * E:], start=True, stop=True).then_inc(s_mm, 1)
                    wait(e, d_i, 16)
                    wait(e, s_rows, 1)
                    for b in range(B):
                        mm = e.matmul(ps[:, 4 + b // TB, b % TB * E:(b % TB + 1) * E],
                                      ident[0:B, b:b + 1].to_broadcast([B, P]), rows4[:, 0, :], start=True, stop=True)
                    mm.then_inc(s_gb, 1)

                    for b in range(B):
                        wait(e, s_xh, b + 1)
                        wait(e, s_ht, b - 1)
                        for t in range(TB):
                            mm = e.transpose(ps[:, b % 2, t * P:(t + 1) * P], xh[:, b % 2, t, :], ident[:])
                        mm.then_inc(s_tr, 1)

                @block.vector
                def _(e):
                    step = chain(e, s_dve)
                    wait(e, s_exp, 1)
                    step(e.tensor_scalar(ct[:, 1, :], ct[:, 1, :], 1.0, None, ALU.add))
                    step(e.reciprocal(ct[:, 2, :], ct[:, 1, :]))
                    e.tensor_tensor(ct[:, 1, :], ct[:, 0, :], ct[:, 2, :], op=ALU.mult).then_inc(s_silu, 1)
                    def tile_stats(first, last):
                        for n in range(first, last):
                            if n % NQ == 0:
                                wait(e, d_x[n // NQ], 16)
                            e.bn_stats(stats[:, n, :], x_all[:, n, :]).then_inc(s_st, 1)
                    tile_stats(0, NT // 2)
                    wait(e, s_mm, 3)
                    e.tensor_copy(mod1[:, 0, :], ps[:, 3, 0:B]).then_inc(s_mod, 1)
                    e.tensor_scalar(mod1[:, 1, :], ps[:, 3, B:2 * B], 1.0, None, ALU.add).then_inc(s_mod, 1)
                    step(e.tensor_copy(rows4[:].rearrange("b k f -> b (k f)"), ps[0:B, 2, :]))
                    step(e.tensor_scalar(rows4[:, 2, :], rows4[:, 2, :], 1.0, None, ALU.add))
                    for m in (0, 3):
                        src = rows4[:, m, :]
                        step(e.tensor_scalar(gt[:, 0], src, 0.0, 2.0, ALU.is_ge, ALU.mult),
                             e.scalar_tensor_tensor(out=gt[:, 1], in0=src, scalar=-1.0, in1=src,
                                                    op0=ALU.mult, op1=ALU.max))
                        step(e.tensor_scalar(gt[:, 0], gt[:, 0], -1.0, None, ALU.add))
                        ins = e.scalar_tensor_tensor(out=src, in0=gt[:, 1], scalar=0.25, in1=gt[:, 0],
                                                     op0=ALU.max, op1=ALU.mult)
                        if m == 0:
                            step(ins)
                        else:
                            ins.then_inc(s_rows, 1)
                    group_begin(e, step, 0, s_st, s_var)
                    wait(e, s_var, 1)
                    group_end(e, step, 0, s_root)
                    tile_stats(NT // 2, NT)
                    group_begin(e, step, 1, s_st, s_var)

                    for b in range(B + 2):
                        if b < B:
                            wait(e, s_tr, b - 1)
                            normalise(e, b, xh[:, b % 2]).then_inc(s_xh, 1)
                        if b >= 2:
                            wait(e, s_ht, b - 1)
                            e.tensor_copy(h_hi[:, (b - 2) * S:(b - 1) * S], ht[:, (b - 2) % RING, :]).then_inc(s_hi, 1)
                        if (b + 1) * TB == GROUPS[1][0]:
                            group_end(e, step, 1, s_root)
                    wait(e, d_i, 16)
                    wait(e, d_k, 16)
                    step(e.tensor_copy(ident_b[:], ident[:]), e.tensor_copy(mask_b[:], mask_f[:]))

                @block.gpsimd
                def _(e):
                    for i, number in enumerate(NUMBERS):
                        e.memset(numbers[:, i, :], number).then_inc(s_num, 1)
                    e.memset(pause[:], 0.0).then_inc(s_num, 1)
                    wait(e, s_num, 6)
                    wait(e, s_whi, 1)
                    e.tensor_tensor(wq_lo[:], wq_f[:], wq_hi[:], op=ALU.subtract).then_inc(s_wlo, 1)
                    low_parts(e, ht, s_hi, s_lo)

        with ExitStack() as ph:
            raw = [sb(ph, f"raw{p}", [P, TB, 384]) for p in range(4)]
            rot = sb(ph, "rot", [P, TB, 256])
            qk = [sb(ph, f"qk{p}", [P, TB, 256]) for p in range(2)]
            qt = [[sb(ph, f"qt{p}{q}", [P, S], F32R) for q in "hl"] for p in range(2)]
            kt = [[sb(ph, f"kt{p}{q}", [P, S], F32R) for q in "hl"] for p in range(2)]
            prob = sb(ph, "prob", [P, 4, S])
            probt = [sb(ph, f"probt{p}", [P, 2, TB, S]) for p in range(2)]
            nmax = sb(ph, "nmax", [P, 2, NU])
            den = sb(ph, "den", [P, 2, NU])
            rden = sb(ph, "rden", [P, NU])
            rrep = sb(ph, "rrep", [P, TB, 2, HD])
            ones = sb(ph, "ones", [P, NU])
            wog = sb(ph, "wog", [P, E])
            ot = sb(ph, "ot", [P, S])
            (p_prj, p_tr, p_s, p_pt, p_o, p_r, p_out, a_raw, a_hi, a_exp, a_pt, a_r,
             v_max, v_pt, v_cos, v_lo, v_rden, v_ot, v_acc, g_sin, g_rot, g_rep, g_one, g_wo) = (
                sem("b_" + n) for n in (
                    "prj", "tr", "s", "pt", "o", "r", "out", "araw", "ahi", "aexp", "apt",
                    "ar", "vmax", "vpt", "vcos", "vlo", "vrden", "vot", "vacc", "gsin", "grot", "grep", "gone",
                    "gwo"))
            bank_s, bank_pt, bank_o, bank_r = 2, 4, 6, 7
            BY_ACT = (0, 1, 3, 5, 7)

            def width(u):
                return (UNITS[u][1] + 1) * P

            def stored(n, u):
                mine = [x for x in range(NU) if (x in BY_ACT) == (u in BY_ACT)]
                return (a_pt if u in BY_ACT else v_pt), len(mine) * n + mine.index(u) + 1

            def work_bank(k):
                return ps[:, k % 2, :]

            def pe_project(e, n, par, t):
                nxt = par % 2
                if t == 0:
                    wait(e, s_hb[nxt], 16 * (n + 2 - nxt) + 32)
                if t < 2:
                    wait(e, v_lo, 2 * n + 1 + t)
                    if isinstance(n, int) and n == -1:
                        wait(e, a_raw, t + 3)
                else:
                    wait(e, a_raw, 4 * (n + 2) + t - 1)
                o = work_bank(t)[:, 0:384]
                cols = bass.ds(((n + 2) % HP) * 384, 384)
                hi, lo = (hb[nxt][q][:, t * P:(t + 1) * P] for q in range(2))
                e.matmul(o, hi, wq_hi[:, cols], start=True, stop=False)
                e.matmul(o, hi, wq_lo[:, cols], start=False, stop=False)
                e.matmul(o, lo, wq_hi[:, cols], start=False, stop=True).then_inc(p_prj, 1)

            def pe_turn(e, n, par, which):
                if which == 0:
                    wait(e, g_rot, 2 * (n + 2))
                if not isinstance(n, int) or n + 2 < STEPS:
                    wait(e, a_raw, 4 * (n + 2) + 3 + which)
                for t in range(TB):
                    mm = e.transpose(work_bank(which)[:, t * P:(t + 1) * P],
                                     qk[(par + 1) % 2][:, t, which * P:(which + 1) * P], ident[:])
                mm.then_inc(p_tr, 1)

            def pe_scores(e, n, par, u):
                g = NU * n + u
                if u == 0:
                    wait(e, v_lo, 2 * n + 2)
                wait(e, a_exp, g - 1)
                j, i = UNITS[u]
                w = width(u)
                o = ps[:, bank_s + u % 2, 0:w]
                par = par % 2
                rows = slice(j * HD, (j + 1) * HD)
                cols = slice(i * P, (i + 1) * P)
                e.matmul(o, qt[par][0][rows, cols], kt[par][0][rows, 0:w], start=True, stop=False)
                e.matmul(o, qt[par][1][rows, cols], kt[par][0][rows, 0:w], start=False, stop=False)
                e.matmul(o, qt[par][0][rows, cols], kt[par][1][rows, 0:w], start=False, stop=False)
                e.matmul(ps[:, bank_s + u % 2, w - P:w], ident_b[:], mask_b[:], start=False,
                         stop=True).then_inc(p_s, 1)

            def pe_turn_prob(e, n, u):
                wait(e, a_exp, NU * n + u + 1)
                wait(e, *(stored(n, u - 2) if u >= 2 else stored(n - 1, NU + u - 2)))
                for kk in range(UNITS[u][1] + 1):
                    mm = e.transpose(ps[:, bank_pt + u % 2, kk * P:(kk + 1) * P],
                                     prob[:, u % 4, kk * P:(kk + 1) * P], ident[:])
                mm.then_inc(p_pt, 1)

            def pe_values(e, n, par):
                wait(e, v_pt, (NU - len(BY_ACT)) * (n + 1))
                wait(e, a_pt, len(BY_ACT) * (n + 1))
                wait(e, v_ot, n)
                for kk in range(TB):
                    for j in range(2):
                        mm = e.matmul(ps[j * HD:(j + 1) * HD, bank_o, kk * P:S],
                                      raw[par][:, kk, 256 + j * HD:256 + (j + 1) * HD],
                                      probt[par % 2][:, j, kk, kk * P:S], start=(kk == 0), stop=(kk == TB - 1))
                mm.then_inc(p_o, 1)

            def pe_turn_sum(e, n):
                wait(e, g_rep, n + 1)
                wait(e, v_acc, n)
                for i in range(TB):
                    mm = e.transpose(ps[:, bank_r, i * P:(i + 1) * P],
                                     rrep[:, i, :, :].rearrange("p j f -> p (j f)"), ident[:])
                mm.then_inc(p_r, 1)

            def pe_out(e, n):
                wait(e, g_wo, n + 1)
                wait(e, v_ot, n + 1)
                for t in range(TB):
                    mm = e.matmul(ps[:, bank_r, t * P:(t + 1) * P], ot[:, t * P:(t + 1) * P],
                                  wog[:], start=True, stop=True)
                mm.then_inc(p_out, 1)

            BEFORE, NOW, AFTER, AFTER2 = range(4)

            def run(e, table, parts, n, par, when):
                for what, arg, of in table:
                    if when[of]:
                        parts[what](e, n, par, arg)

            PE_ORDER = [("project", 0, AFTER2), ("scores", 0, NOW), ("project", 1, AFTER2),
                        ("turn_prob'", 5, BEFORE), ("scores", 1, NOW), ("turn_prob'", 6, BEFORE),
                        ("turn_prob'", 7, BEFORE), ("turn_sum", 0, BEFORE), ("project", 2, AFTER2),
                        ("scores", 2, NOW), ("turn_prob", 0, NOW), ("scores", 3, NOW), ("project", 3, AFTER2),
                        ("turn", 0, AFTER), ("turn_prob", 1, NOW), ("turn_prob", 2, NOW), ("scores", 4, NOW),
                        ("scores", 5, NOW), ("values", 0, BEFORE), ("turn_prob", 3, NOW), ("scores", 6, NOW),
                        ("turn", 1, AFTER), ("scores", 7, NOW), ("turn_prob", 4, NOW), ("out", 0, BEFORE)]
            PE_PARTS = {
                "turn_prob'": lambda e, n, par, u: pe_turn_prob(e, n - 1, u),
                "turn_prob": lambda e, n, par, u: pe_turn_prob(e, n, u),
                "values": lambda e, n, par, _: pe_values(e, n - 1, (par + 3) % 4),
                "scores": pe_scores,
                "project": pe_project,
                "turn_sum": lambda e, n, par, _: pe_turn_sum(e, n - 1),
                "out": lambda e, n, par, _: pe_out(e, n - 1),
                "turn": pe_turn}

            def act_raw(e, n, par, t):
                m = n + 2
                wait(e, p_prj, 4 * m + t + 1)
                if t == 0:
                    wait(e, p_o, n - 1)
                e.copy(raw[(par + 2) % 4][:, t, :], work_bank(t)[:, 0:384]).then_inc(a_raw, 1)

            def act_hi(e, n, par, which):
                wait(e, p_tr, 2 * (n + 1) + which + 1)
                if which == 0:
                    wait(e, p_s, NU * n)
                dst = (qt, kt)[which][(par + 1) % 2][0]
                e.copy(dst[:], work_bank(which)).then_inc(a_hi, 1)

            def act_exp(e, n, par, u):
                g = NU * n + u
                j, i = UNITS[u]
                wait(e, v_max, g + 1)
                wait(e, p_pt, g - 3)
                if u == 0:
                    wait(e, v_rden, n - 1)
                e.activation(prob[:, u % 4, 0:width(u)], ps[:, bank_s + u % 2, 0:width(u)], ACT.Exp,
                             bias=nmax[:, par % 2, u:u + 1],
                             accum_out=den[:, par % 2, 2 * i + j:2 * i + j + 1]).then_inc(a_exp, 1)

            def store_prob(e, n, par, u, copy):
                j, i = UNITS[u]
                wait(e, p_pt, NU * n + u + 1)
                if u < 2:
                    wait(e, p_o, n - 1)
                copy(probt[par % 2][:, j, 0:i + 1, i * P:(i + 1) * P],
                     ps[:, bank_pt + u % 2, 0:width(u)].rearrange("p (k q) -> p k q", q=P))\
                    .then_inc(stored(0, u)[0], 1)

            def act_r(e, n):
                wait(e, p_r, n + 1)
                wait(e, p_out, n)
                e.copy(ot[:], ps[:, bank_r, :]).then_inc(a_r, 1)

            ACT_ORDER = [("raw", 0, AFTER2), ("store'", 5, BEFORE), ("raw", 1, AFTER2), ("exp", 0, NOW),
                         ("exp", 1, NOW), ("store'", 7, BEFORE), ("raw", 2, AFTER2), ("store", 0, NOW),
                         ("exp", 2, NOW), ("exp", 3, NOW), ("store", 1, NOW), ("hi", 0, AFTER), ("raw", 3, AFTER2),
                         ("exp", 4, NOW), ("sum", 0, BEFORE), ("exp", 5, NOW), ("hi", 1, AFTER), ("exp", 6, NOW),
                         ("exp", 7, NOW), ("store", 3, NOW)]
            ACT_PARTS = {
                "store'": lambda e, n, par, u: store_prob(e, n - 1, (par + 3) % 4, u, e.copy),
                "store": lambda e, n, par, u: store_prob(e, n, par, u, e.copy),
                "exp": act_exp,
                "raw": act_raw,
                "sum": lambda e, n, par, _: act_r(e, n - 1),
                "hi": act_hi}

            def dve_max(e, n, par, u):
                wait(e, p_s, NU * n + u + 1)
                e.tensor_reduce(nmax[:, par % 2, u:u + 1], ps[:, bank_s + u % 2, 0:width(u)], AX.X, ALU.max,
                                negate=True).then_inc(v_max, 1)

            def dve_cos(e, n, par, half):
                m = n + 2
                wait(e, a_raw, 4 * m + 2 * half + 2)
                wait(e, p_tr, 2 * (n + 1))
                t = slice(2 * half, 2 * half + 2)
                e.tensor_tensor(qk[par % 2][:, t, :], raw[(par + 2) % 4][:, t, 0:256], cos[:, t, :], op=ALU.mult).then_inc(v_cos, 1)

            def dve_lo(e, n, par, which):
                wait(e, a_hi, 2 * (n + 1) + which + 1)
                hi, lo = (qt, kt)[which][(par + 1) % 2]
                e.tensor_tensor(lo[:], work_bank(which), hi[:], op=ALU.subtract).then_inc(v_lo, 1)

            def dve_rden(e, n, par):
                wait(e, a_exp, NU * (n + 1))
                wait(e, g_rep, n)
                e.reciprocal(rden[:], den[:, par % 2, :]).then_inc(v_rden, 1)

            def dve_ot(e, n):
                wait(e, a_r, n + 1)
                wait(e, p_o, n + 1)
                e.tensor_tensor(ot[:], ps[:, bank_o, :], ot[:], op=ALU.mult).then_inc(v_ot, 1)

            def dve_acc(e, n):
                wait(e, p_out, n + 1)
                wait(e, v_acc, n)
                dst = x_all[:, bass.ds((n // HP) * TB, TB), :]
                e.tensor_tensor(dst, ps[:, bank_r, :].rearrange("p (t f) -> p t f", t=TB), dst,
                                op=ALU.add).then_inc(v_acc, 1)

            DVE_ORDER = [("rden", 0, BEFORE), ("max", 0, NOW), ("store'", 4, BEFORE), ("max", 1, NOW),
                         ("store'", 6, BEFORE), ("max", 2, NOW), ("cos", 0, AFTER2), ("max", 3, NOW),
                         ("max", 4, NOW), ("lo", 0, AFTER), ("max", 5, NOW), ("ot", 0, BEFORE), ("store", 2, NOW),
                         ("cos", 1, AFTER2), ("max", 6, NOW), ("lo", 1, AFTER), ("max", 7, NOW), ("acc", 0, BEFORE)]
            DVE_PARTS = {
                "rden": lambda e, n, par, _: dve_rden(e, n - 1, (par + 3) % 4),
                "store'": lambda e, n, par, u: store_prob(e, n - 1, (par + 3) % 4, u, e.tensor_copy),
                "store": lambda e, n, par, u: store_prob(e, n, par, u, e.tensor_copy),
                "max": dve_max,
                "cos": dve_cos,
                "ot": lambda e, n, par, _: dve_ot(e, n - 1),
                "acc": lambda e, n, par, _: dve_acc(e, n - 1),
                "lo": dve_lo}

            def pool_rep(e, n):
                wait(e, v_rden, n + 1)
                wait(e, p_r, n)
                e.tensor_tensor(rrep[:].rearrange("p t j f -> p (t j) f"),
                                rden[:].unsqueeze(2).to_broadcast([P, NU, HD]),
                                ones[:].unsqueeze(2).to_broadcast([P, NU, HD]), op=ALU.mult).then_inc(g_rep, 1)

            def pool_rotate(e, n, par, half):
                m = n + 2
                t = slice(2 * half, 2 * half + 2)

                def part(x, k, width=256):
                    return x[:, t, 0:256].rearrange("p t (h k f) -> p t h k f", k=2, f=HD // 2)[:, :, :, k, :]
                wait(e, a_raw, 4 * m + 2 * half + 2)
                wait(e, g_rot, 2 * m - 1 + half)
                for k in range(2):
                    e.tensor_tensor(part(rot, k), part(raw[(par + 2) % 4], 1 - k), part(sin, k), op=ALU.mult)\
                        .then_inc(g_sin, 1)
                wait(e, v_cos, 2 * m + half + 1)
                wait(e, g_sin, 4 * m + 2 * half + 2)
                e.tensor_tensor(qk[par % 2][:, t, :], qk[par % 2][:, t, :], rot[:, t, :], op=ALU.add).then_inc(g_rot, 1)

            def pool_wo(e, n):
                wait(e, p_out, n)
                e.tensor_tensor(wog[:], wo[:, bass.ds((n % HP) * E, E)],
                                ga[:, bass.ds(n // HP, 1), :].rearrange("p a f -> p (a f)"),
                                op=ALU.mult).then_inc(g_wo, 1)

            POOL_ORDER = [("rep", 0, BEFORE), ("wo", 0, BEFORE), ("rotate", 0, AFTER2), ("rotate", 1, AFTER2)]
            POOL_PARTS = {
                "rep": lambda e, n, par, _: pool_rep(e, n - 1),
                "wo": lambda e, n, par, _: pool_wo(e, n - 1),
                "rotate": pool_rotate}

            def all_steps(e, table, parts):
                whole = (True, True, True, True)
                run(e, table, parts, -2, 2, (False, False, False, True))
                run(e, table, parts, -1, 3, (False, False, True, True))
                run(e, table, parts, 0, 0, (False, True, True, True))
                run(e, table, parts, 1, 1, whole)
                with e.Fori(0, (STEPS - 4) // 4) as i:
                    for j in range(4):
                        run(e, table, parts, 4 * i + 2 + j, (2 + j) % 4, whole)
                run(e, table, parts, STEPS - 2, 2, (True, True, True, False))
                run(e, table, parts, STEPS - 1, 3, (True, True, False, False))
                run(e, table, parts, STEPS, 0, (True, False, False, False))

            with nc.Block() as block:
                @block.sync
                def _(e):
                    def load(m, par):
                        cols = bass.ds(e.snap((m // HP) * S) if not isinstance(m, int) else (m // HP) * S, S)
                        wait(e, p_prj, 4 * (m - 1))
                        load_h(e, cols, par)
                    e.dma_start(w_raw[:], w_up[:, 0:WH]).then_inc(d_e[0], 16)
                    with e.Fori(1, STEPS // 2) as i:
                        load(2 * i, 0)
                        load(2 * i + 1, 1)

                @block.tensor
                def _(e):
                    all_steps(e, PE_ORDER, PE_PARTS)

                @block.scalar
                def _(e):
                    all_steps(e, ACT_ORDER, ACT_PARTS)

                @block.vector
                def _(e):
                    wait(e, d_late, 48)
                    all_steps(e, DVE_ORDER, DVE_PARTS)

                @block.gpsimd
                def _(e):
                    e.memset(ones[:], 1.0).then_inc(g_one, 1)
                    wait(e, g_one, 1)
                    wait(e, d_late, 48)
                    all_steps(e, POOL_ORDER, POOL_PARTS)
        att.close()

        ffn = ctx.enter_context(ExitStack())
        mod = sb(ffn, "mod", [P, B, 3, E])
        logits = sb(ffn, "logits", [P, NT, NX])
        share = sb(ffn, "share", [P, NT, NX])
        expo = sb(ffn, "expo", [P, NT, NX])
        r8 = sb(ffn, "r8", [P, 2, NT, NX])
        r1 = sb(ffn, "r1", [P, 4, NT])
        best, place, total, under = (r1[:, i, :] for i in range(4))
        rank = sb(ffn, "rank", [P, NX])
        w_raw2 = sb(ffn, "w_raw2", [P, 2, WH])
        w1_lo, w3_hi, w3_lo = sem("w1_lo"), sem("w3_hi"), sem("w3_lo")

        def over(a):
            return a.unsqueeze(2).to_broadcast([P, NT, NX])

        def part(q):
            cols = slice(q % 2 * WH, (q % 2 + 1) * WH)
            return (w_raw[:], w_raw2[:, 0, :], w_raw2[:, 1, :], w_raw[:])[q], (wu, wd)[q // 2][0][:, cols], (wu, wd)[q // 2][1][:, cols]

        def low_weight(e, q, done):
            raw_, hi, lo = part(q)
            e.tensor_tensor(lo, raw_, hi, op=ALU.subtract).then_inc(done, 1)
        wu = [sb(ffn, f"wu{q}", [P, NX * I], F32R) for q in "hl"]
        wd = [sb(ffn, f"wd{q}", [P, NX * IC * E], F32R) for q in "hl"]
        with ExitStack() as ph:
            gate_sb = sb(ph, "gate_sb", [P, NX])
            bias_sb = sb(ph, "bias_sb", [P, NX])
            rows_part = [sb(ph, f"rows_{q}", [B, 3 * E], F32R) for q in "hl"]
            ident_r = sb(ph, "ident_r", [B, B], F32R)
            s_part = sem("c_part")
            modt = sb(ph, "modt", [P, 2, B])
            xh = sb(ph, "xh3", [P, 2, TB, E])
            ht = sb(ph, "ht3", [P, RING, S])
            (d_k, s_st, s_dve, s_var, s_root, s_rt, s_rtc, s_mb, s_mbc, s_xh, s_tr, s_hi, s_ht, s_lo, s_lg, s_lgs,
             s_whi, s_wlo) = (
                sem("c_" + n) for n in ("dk", "st", "dve", "var", "root", "rt", "rtc", "mb", "mbc", "xh", "tr", "hi",
                                        "ht", "lo", "lg", "lgs", "whi", "wlo"))

            with nc.Block() as block:
                @block.sync
                def _(e):
                    e.dma_start(part(2)[0], w_down[:, 0:WH]).then_inc(d_e[2], 16)
                    e.dma_start(gate_sb[:], gate_w).then_inc(d_k, 16)
                    e.dma_start(rank[:], rank_in).then_inc(d_k, 16)
                    e.dma_start(bias_sb[:], expert_bias.partition_broadcast(P)).then_inc(d_k, 16)
                    e.dma_start(part(1)[0], w_up[:, WH:]).then_inc(d_e[1], 16)
                    wait(e, s_wlo, 1)
                    e.dma_start(w_raw[:], w_down[:, WH:]).then_inc(d_e[3], 16)

                @block.gpsimd
                def _(e):
                    for i, q in enumerate((0, 2)):
                        wait(e, s_whi, i + 1)
                        low_weight(e, q, s_wlo)
                    low_parts(e, ht, s_hi, s_lo)

                @block.scalar
                def _(e):
                    def high(q):
                        raw_, hi, lo = part(q)
                        wait(e, d_e[q], 16)
                        e.copy(hi, raw_).then_inc(s_whi, 1)
                    wait(e, s_rt, 1)
                    e.copy(modt[:].rearrange("p k b -> p (k b)"), ps[:, 7, 0:2 * B]).then_inc(s_rtc, 1)
                    group_root(e, 0, s_var, s_root)
                    high(0)

                    def spread(first, last):
                        for b in range(first, last):
                            wait(e, s_mb, b + 1)
                            e.copy(mod[:, b, :, :].rearrange("p k f -> p (k f)"), ps[:, 4 + b % 3, 0:3 * E])\
                                .then_inc(s_mbc, 1)
                    spread(0, 5)
                    group_root(e, 1, s_var, s_root)
                    spread(5, B)
                    high(2)
                    wait(e, s_rtc, 1)
                    for b in range(B):
                        wait(e, s_tr, b + 1)
                        wait(e, s_lo, b - RING + 1)
                        wait(e, s_lg, b - RING + 1)
                        e.activation(ht[:, b % RING, :], ps[:, b % 2, :], ACT.Identity, bias=modt[:, 0, b:b + 1],
                                     scale=modt[:, 1, b:b + 1]).then_inc(s_ht, 1)
                    high(1)

                @block.tensor
                def _(e):
                    for i in range(2):
                        mm = e.transpose(ps[:, 7, i * B:(i + 1) * B], rows4[:, 1 + i, :], ident[0:B, 0:B])
                    mm.then_inc(s_rt, 1)

                    wait(e, s_part, 3)
                    for b in range(B):
                        wait(e, s_mbc, b - 2)
                        for q in range(2):
                            mm = e.matmul(ps[:, 4 + b % 3, 0:3 * E], ident_r[:, b:b + 1].to_broadcast([B, P]),
                                          rows_part[q][:], start=(q == 0), stop=(q == 1))
                        mm.then_inc(s_mb, 1)

                    wait(e, d_k, 48)
                    for b in range(B + 1):
                        if b < B:
                            wait(e, s_xh, b + 1)
                            wait(e, s_ht, b - 1)
                            for t in range(TB):
                                mm = e.transpose(ps[:, b % 2, t * P:(t + 1) * P], xh[:, b % 2, t, :], ident[:])
                            mm.then_inc(s_tr, 1)
                        if b >= 1:
                            wait(e, s_ht, b)
                            for t in range(TB):
                                n = (b - 1) * TB + t
                                mm = e.matmul(ps[:, 2, n * NX:(n + 1) * NX],
                                              ht[:, (b - 1) % RING, t * P:(t + 1) * P], gate_sb[:], start=True, stop=True)
                            mm.then_inc(s_lg, 1)

                @block.vector
                def _(e):
                    step = chain(e, s_dve)

                    last3 = rows4[:, 1:4, :].rearrange("b k f -> b (k f)")
                    e.tensor_copy(rows_part[0][:], last3).then_inc(s_part, 1)
                    e.tensor_copy(ident_r[:], ident[0:B, 0:B]).then_inc(s_part, 1)
                    wait(e, s_part, 2)
                    e.tensor_tensor(rows_part[1][:], last3, rows_part[0][:], op=ALU.subtract).then_inc(s_part, 1)
                    for g, (first, last) in enumerate(GROUPS):
                        for n in range(first, last):
                            e.bn_stats(stats[:, n, :], x_all[:, n, :]).then_inc(s_st, 1)
                        group_begin(e, step, g, s_st, s_var)
                    wait(e, s_var, 2)
                    group_end(e, step, 0, s_root)
                    wait(e, d_k, 48)

                    for b in range(B + 2):
                        if b < B:
                            wait(e, s_tr, b - 1)
                            normalise(e, b, xh[:, b % 2]).then_inc(s_xh, 1)
                        if b >= 2:
                            wait(e, s_ht, b - 1)
                            e.tensor_copy(h_hi[:, (b - 2) * S:(b - 1) * S], ht[:, (b - 2) % RING, :]).then_inc(s_hi, 1)
                        if (b + 1) * TB == GROUPS[1][0]:
                            group_end(e, step, 1, s_root)
                    wait(e, s_lg, B)
                    e.tensor_tensor(logits[:], ps[:, 2, 0:NT * NX].rearrange("p (t x) -> p t x", x=NX),
                                    bias_sb[:].unsqueeze(1).to_broadcast([P, NT, NX]), op=ALU.add).then_inc(s_lgs, 1)

        with ExitStack() as ph:
            NC = NX * IC
            hf = sb(ph, "hf", [P, 4, S])
            hh = sb(ph, "hh", [P, 4, S], F32R)
            hl = sb(ph, "hl", [P, 4, S], F32R)
            st4 = sb(ph, "st4", [P, TB, 6])
            m4 = sb(ph, "m4", [P, TB])
            r4 = sb(ph, "r4", [P, TB])
            t4 = sb(ph, "t4", [P, 3, TB])
            acc = sb(ph, "acc", [P, NT, E])
            h2 = sb(ph, "h2", [P, TB, E])
            y4 = sb(ph, "y4", [P, TB, E])
            yt = sb(ph, "yt", [P, 2, S])
            (p_up, p_dn, p_ty, a_y, a_ge, a_hi, v_hi, v_lo, v_acc, v_st, v_y, v_xh, g_nf, g_f, g_h, g_y, d_out) = (
                sem("d_" + n) for n in ("up", "dn", "ty", "ay", "ge", "ahi", "hi", "lo", "acc", "st", "y", "vxh", "gnf", "gf", "gh", "gy", "out"))
            s_rt, s_top, s_e, g_lo, v_end, v_var, v_out, a_root = (
                sem("d_" + n) for n in ("rt", "top", "e", "glo", "end", "var", "vout", "root"))
            root4 = sb(ph, "root4", [P, TB])
            LAG = 3
            BY_POOL = 7

            def low_part(n, k):
                if isinstance(n, int) and n == 0 and k < BY_POOL:
                    return g_lo, k + 1
                return v_lo, NC * n + k + 1 - BY_POOL

            def router(e):
                rk = rank[:].unsqueeze(1).to_broadcast([P, NT, NX])
                first, t = r8[:, 0], r8[:, 1]
                step = chain(e, s_rt)
                step(e.tensor_reduce(best, logits[:], AX.X, ALU.max))
                e.tensor_tensor(first, logits[:], over(best), op=ALU.subtract).then_inc(s_top, 1)
                wait(e, s_e, 1)
                step(e.tensor_reduce(total, expo[:], AX.X, ALU.add),
                     e.scalar_tensor_tensor(out=t, in0=expo[:], scalar=1.0, in1=rk, op0=ALU.is_equal, op1=ALU.mult))
                step(e.tensor_reduce(place, t, AX.X, ALU.max))
                step(e.tensor_tensor(first, rk, over(place), op=ALU.is_equal))
                step(e.scalar_tensor_tensor(out=expo[:], in0=first, scalar=-2.0, in1=expo[:], op0=ALU.mult, op1=ALU.add))
                step(e.tensor_reduce(best, expo[:], AX.X, ALU.max))
                step(e.tensor_tensor(t, expo[:], over(best), op=ALU.is_equal),
                     e.scalar_tensor_tensor(out=under, in0=total, scalar=GATE_EPS, in1=best, op0=ALU.mult, op1=ALU.add))
                step(e.tensor_tensor(t, t, rk, op=ALU.mult),
                     e.tensor_scalar(under, under, 1.0, None, ALU.add))
                step(e.tensor_reduce(place, t, AX.X, ALU.max),
                     e.reciprocal(total, under))
                step(e.tensor_tensor(t, rk, over(place), op=ALU.is_equal))
                step(e.tensor_tensor(t, t, over(best), op=ALU.mult))
                step(e.tensor_tensor(t, t, first, op=ALU.add))
                step(e.tensor_tensor(share[:], t, over(total), op=ALU.mult))

            bank_y, bank_t = 4, 6

            def up(e, n, k):
                g = NC * n + k
                wait(e, a_ge, g - 3)
                if isinstance(n, int) and n == 0 and k == NC // 2:
                    wait(e, w1_lo, 1)
                o = ps[:, k % 4, :]
                w = slice(k * P, (k + 1) * P)
                cols = bass.ds(n * S, S)
                e.matmul(o, wu[0][:, w], h_hi[:, cols], start=True, stop=False)
                e.matmul(o, wu[0][:, w], h_lo[:, cols], start=False, stop=False)
                e.matmul(o, wu[1][:, w], h_hi[:, cols], start=False, stop=True).then_inc(p_up, 1)

            def down(e, n, k):
                g = NC * n + k
                x, c = divmod(k, IC)
                wait(e, *low_part(n, k))
                if isinstance(n, int) and n == 0 and k == NC // 2:
                    wait(e, w3_hi, 1)
                    wait(e, w3_lo, 1)
                if c == 0:
                    wait(e, a_y, NX * n + x - 1)
                w = slice(k * E, (k + 1) * E)
                o = ps[:, bank_y + x % 2, :]
                e.matmul(o, wd[0][:, w], hh[:, k % 4, :], start=(c == 0), stop=False)
                e.matmul(o, wd[0][:, w], hl[:, k % 4, :], start=False, stop=False)
                e.matmul(o, wd[1][:, w], hh[:, k % 4, :], start=False, stop=(c == IC - 1)).then_inc(p_dn, 1)

            def turn_y(e, n, x):
                wait(e, a_y, NX * n + x + 1)
                wait(e, v_acc, NX * n + x - 1)
                for t in range(TB):
                    mm = e.transpose(ps[:, bank_t + x % 2, t * P:(t + 1) * P], yt[:, x % 2, t * P:(t + 1) * P],
                                     ident[:])
                mm.then_inc(p_ty, 1)

            def each(k, lag, now, before, n, act):
                q = k - lag
                if q % IC == IC - 1:
                    if q >= 0 and now:
                        act(n, q // IC)
                    if q < 0 and before:
                        act(n - 1, NX + q // IC)

            def pe4(e, n, now=True, before=True):
                for k in range(NC):
                    if now:
                        up(e, n, k)
                    if k >= LAG:
                        if now:
                            down(e, n, k - LAG)
                    elif before:
                        down(e, n - 1, NC - LAG + k)
                    each(k, LAG + 2, now, before, n, lambda m, x: turn_y(e, m, x))

            def store_y(e, n, x):
                wait(e, p_dn, NC * n + IC * (x + 1))
                wait(e, p_ty, NX * n + x - 1)
                e.copy(yt[:, x % 2, :], ps[:, bank_y + x % 2, :]).then_inc(a_y, 1)

            def act4(e, n, now=True, before=True):
                for k in range(NC):
                    if now:
                        g = NC * n + k
                        wait(e, p_up, g + 1)
                        if not isinstance(n, int) or n > 0 or k >= 4:
                            back = (n, k - 4) if k >= 4 else (n - 1, NC + k - 4)
                            wait(e, *low_part(*back))
                        e.activation(hf[:, k % 4, :], ps[:, k % 4, :], ACT.Gelu).then_inc(a_ge, 1)
                        if isinstance(n, int) and n == 0 and k == BY_POOL - 1:
                            wait(e, d_e[3], 16)
                            e.copy(part(3)[1], part(3)[0]).then_inc(w3_hi, 1)
                        if k % 2 or (isinstance(n, int) and n == 0 and k < BY_POOL):
                            wait(e, a_ge, g + 1)
                            wait(e, p_dn, g - 3)
                            e.copy(hh[:, k % 4, :], hf[:, k % 4, :]).then_inc(a_hi, 1)
                    each(k, LAG + 1, now, before, n, lambda m, x: store_y(e, m, x))
                if not now:
                    wait(e, v_var, 1)
                    e.activation(root4[:], t4[:, 1, :], ACT.Sqrt).then_inc(a_root, 1)

            def add_up(e, n, x):
                wait(e, p_ty, NX * n + x + 1)
                wait(e, v_acc, NX * n + x)
                for t in range(TB):
                    dst = acc[:, bass.ds(n * TB + t, 1), :].rearrange("p a f -> p (a f)")
                    src = ps[:, bank_t + x % 2, t * P:(t + 1) * P]
                    wt = share[:, bass.ds(n * TB + t, 1), x:x + 1].rearrange("p a f -> p (a f)")
                    if x == 0:
                        ins = e.tensor_scalar(dst, src, wt, None, ALU.mult)
                    else:
                        ins = e.scalar_tensor_tensor(out=dst, in0=src, scalar=wt, in1=dst, op0=ALU.mult, op1=ALU.add)
                ins.then_inc(v_acc, 1)

            def dve4(e, n, now=True, before=True):
                for k in range(NC):
                    if now and k == 0 and isinstance(n, int) and n == 0:
                        router(e)
                    if now and not (isinstance(n, int) and n == 0 and k < BY_POOL):
                        g = NC * n + k
                        extra = (BY_POOL + 1) // 2
                        wait(e, p_dn, g - 3)
                        if k % 2:
                            wait(e, a_hi, (NC // 2) * n + k // 2 + 1 + extra)
                        else:
                            wait(e, a_ge, g + 1)
                            e.tensor_copy(hh[:, k % 4, :], hf[:, k % 4, :]).then_inc(v_hi, 1)
                            wait(e, v_hi, (NC // 2) * n + k // 2 + 1 - extra)
                        e.tensor_tensor(hl[:, k % 4, :], hf[:, k % 4, :], hh[:, k % 4, :],
                                        op=ALU.subtract).then_inc(v_lo, 1)
                    each(k, LAG + 2, now, before, n, lambda m, x: add_up(e, m, x))
                    if before and k == 1:
                        m = n - 1
                        wait(e, g_y, 3 * m)
                        normalise(e, m, h2).then_inc(v_xh, 1)
                    if before and k == 6:
                        m = n - 1
                        wait(e, v_acc, NX * n)
                        e.memset(pause[:, 0:1], 0.0)
                        for t in range(TB):
                            e.bn_stats(st4[:, t, :], acc[:, bass.ds(m * TB + t, 1), :].rearrange("p a f -> p (a f)"))\
                                .then_inc(v_st, 1)
                    if before and k == 6 and not now:
                        last_batch(e)
                    if before and k == 13 and now:
                        m = n - 1
                        wait(e, g_nf, n)
                        wait(e, g_y, 3 * m)
                        for t in range(TB):
                            ts = e.tensor_scalar(y4[:, t, :], acc[:, bass.ds(m * TB + t, 1), :].rearrange("p a f -> p (a f)"),
                                                 m4[:, t:t + 1], r4[:, t:t + 1], ALU.subtract, ALU.mult)
                        ts.then_inc(v_y, 1)

            def last_batch(e):
                m = B - 1
                rows = slice(m * TB, NT)
                step = chain(e, v_end)
                t = [t4[:, i, :] for i in range(3)]
                wait(e, v_st, TB * B)
                wait(e, g_nf, m)
                factors_begin(step, e, lambda k: st4[:, :, k], m4[:], t).then_inc(v_var, 1)
                wait(e, a_root, 1)
                step(factors_end(step, e, r4[:], root4[:], t))
                wait(e, g_y, 3 * m)
                for t in range(TB):
                    ts = e.tensor_scalar(y4[:, t, :], acc[:, m * TB + t, :], m4[:, t:t + 1], r4[:, t:t + 1],
                                         ALU.subtract, ALU.mult)
                step(ts)
                wait(e, g_h, 2 * B)
                step(e.tensor_tensor(y4[:], y4[:], h2[:], op=ALU.add))
                step(e.tensor_tensor(y4[:], y4[:], mod[:, m, 2:3, :].to_broadcast([P, TB, E]), op=ALU.mult))
                e.tensor_tensor(x_all[:, rows, :], x_all[:, rows, :], y4[:], op=ALU.add).then_inc(v_out, 1)

            def pool4(e, m, last=False):
                rows = bass.ds(m * TB, TB)

                def over(k):
                    return mod[:, bass.ds(m, 1), k:k + 1, :].rearrange("p a c f -> p (a c) f")\
                        .to_broadcast([P, TB, E])
                step = chain(e, g_h, 2 * m)
                wait(e, v_xh, m + 1)
                step(e.tensor_tensor(h2[:], h2[:], over(1), op=ALU.mult))
                step(e.tensor_tensor(h2[:], h2[:], over(0), op=ALU.add))
                if last:
                    return
                wait(e, v_st, TB * (m + 1))
                wait(e, v_y, m)
                norm_factors(chain(e, g_f, NORM_STEPS * m), e, lambda k: st4[:, :, k], m4[:], r4[:],
                             [t4[:, i, :] for i in range(3)]).then_inc(g_nf, 1)
                wait(e, v_y, m + 1)
                step = chain(e, g_y, 3 * m)
                step(e.tensor_tensor(y4[:], y4[:], h2[:], op=ALU.add))
                step(e.tensor_tensor(y4[:], y4[:], over(2), op=ALU.mult))
                step(e.tensor_tensor(x_all[:, rows, :], x_all[:, rows, :], y4[:], op=ALU.add))

            def all_batches(e, step):
                step(e, 0, before=False)
                step(e, 1)
                with e.Fori(2, B) as n:
                    step(e, n)
                step(e, B, now=False)

            with nc.Block() as block:
                @block.tensor
                def _(e):
                    all_batches(e, pe4)

                @block.scalar
                def _(e):
                    wait(e, s_top, 1)
                    e.activation(expo[:].rearrange("p n x -> p (n x)"), r8[:, 0].rearrange("p n x -> p (n x)"),
                                 ACT.Exp).then_inc(s_e, 1)
                    all_batches(e, act4)

                @block.vector
                def _(e):
                    all_batches(e, dve4)

                @block.gpsimd
                def _(e):
                    for k in range(BY_POOL):
                        wait(e, a_hi, k + 1)
                        wait(e, p_dn, k - 3)
                        e.tensor_tensor(hl[:, k % 4, :], hf[:, k % 4, :], hh[:, k % 4, :],
                                        op=ALU.subtract).then_inc(g_lo, 1)
                    low_weight(e, 1, w1_lo)
                    wait(e, w3_hi, 1)
                    low_weight(e, 3, w3_lo)
                    pool4(e, 0)
                    with e.Fori(1, B - 1) as m:
                        pool4(e, m)
                    pool4(e, B - 1, last=True)

                @block.sync
                def _(e):
                    ov = out.rearrange("(n p) f -> p n f", p=P)
                    with e.Fori(0, B - 1) as m:
                        wait(e, g_y, 3 * m + 3)
                        e.dma_start(ov[:, bass.ds(m * TB, TB), :], x_all[:, bass.ds(m * TB, TB), :]).then_inc(d_out, 16)
                    wait(e, v_out, 1)
                    e.dma_start(ov[:, NT - TB:, :], x_all[:, NT - TB:, :]).then_inc(d_out, 16)
                    wait(e, d_out, 16 * B)


def kernel(L0_attn_x, L0_attn_W_qkv, L0_attn_W_out, L0_ffn_gate_w, L0_ffn_expert_bias, L0_ffn_w_up, L0_ffn_w_down,
           L0_c, L0_wmod):
    import numpy as np
    import concourse.bacc as bacc
    from concourse.bass_utils import run_bass_kernel_spmd

    w = np.asarray(L0_attn_W_qkv).reshape(E, 3, HP, 2, HD)
    order = np.concatenate([np.arange(0, HD, 2), np.arange(1, HD, 2)])
    w = np.stack([w[:, 0][..., order], w[:, 1][..., order], w[:, 2]], axis=2)
    freqs = (1.0 / np.float32(10000.0) ** (np.arange(0, HD, 2) / HD).astype(np.float32)).astype(np.float32)
    angles = np.arange(S, dtype=np.float32)[:, None] * freqs[None, :]
    co, si = np.cos(angles), np.sin(angles)
    scale = np.repeat(np.array([HD ** -0.5, 1.0], np.float32), 2)[None, :, None]
    cos4 = np.concatenate([co, co], 1)[:, None, :] * scale
    sin4 = np.concatenate([-si, si], 1)[:, None, :] * scale

    def by_tile(a):
        return np.ascontiguousarray(a.reshape(TB, P, 256).transpose(1, 0, 2).reshape(P, TB * 256), np.float32)
    arrays = {
        "x": np.asarray(L0_attn_x).reshape(B * S, E),
        "w_qkv": np.ascontiguousarray(w.reshape(E, HP * 384)),
        "w_out": np.asarray(L0_attn_W_out),
        "gate_w": np.ascontiguousarray(np.asarray(L0_ffn_gate_w).T),
        "expert_bias": np.asarray(L0_ffn_expert_bias),
        "w_up": np.ascontiguousarray(np.asarray(L0_ffn_w_up).transpose(2, 0, 1).reshape(E, NX * I)),
        "w_down": np.ascontiguousarray(np.asarray(L0_ffn_w_down).reshape(NX, E, IC, P).transpose(3, 0, 2, 1)
                                       .reshape(P, NX * IC * E)),
        "c_t": np.ascontiguousarray(np.asarray(L0_c).T),
        "w_mod": np.asarray(L0_wmod),
        "cos": by_tile(cos4),
        "sin": by_tile(sin4),
        "ident": np.eye(P, dtype=np.float32),
        "mask": np.triu(np.full((P, P), MASKED, np.float32), 1),
        "rank": np.tile(np.arange(NX, 0, -1, dtype=np.float32), (P, 1)),
    }
    nc = bacc.Bacc("TRN2", target_bir_lowering=False, num_devices=1)
    args = [nc.dram_tensor("in_" + name, a.shape, mybir.dt.from_np(a.dtype), kind="ExternalInput").ap()
            for name, a in arrays.items()]
    args.append(nc.dram_tensor("out", (B * S, E), F32, kind="ExternalOutput").ap())
    adaln_kernel(nc, *args)
    r = run_bass_kernel_spmd(nc, [{"in_" + name: a for name, a in arrays.items()}], core_ids=[0])
    return r.results[0]["out"].reshape(B, S, E)
```
